# Optimizing a Trainium2 kernel written in Bass

```python
import numpy as np
import jax
import jax.numpy as jnp

def _softmax(x, axis=-1):
    return jax.nn.softmax(x, axis=axis)

def _gelu(x):
    return jax.nn.gelu(x, approximate=True)

def _silu(x):
    return jax.nn.silu(x)

def _sigmoid(x):
    return jax.nn.sigmoid(x)

def _layernorm(x, axis=-1, eps=1e-05):
    m = jnp.mean(x, axis=axis, keepdims=True)
    v = jnp.var(x, axis=axis, keepdims=True)
    return (x - m) / jnp.sqrt(v + eps)

def _scatter_add(tgt, idx, src, axis=0):
    return tgt.at[idx].add(src)

def _segment_sum(src, seg, n):
    return jax.ops.segment_sum(src, seg, n)
kernel_name = 'mk_adj_resnorm_d1_adj_r2_b730fe'

def setup_inputs(seed: int=0):
    np.random.seed(seed)
    _w = jnp.asarray

    def _rec_inputs():
        import jax
        import jax.numpy as jnp
        _gk = jax.random.key(seed)
        x = -0.001003 + 1 * jax.random.normal(jax.random.fold_in(_gk, 1), (8192, 128), jnp.float32)
        _w = (1.0 + jnp.arange(8192, dtype=jnp.float32)) ** (-0.5)
        _w = _w / _w.mean()
        _pij = jnp.clip(0.000488281 * _w[:, None] * _w[None, :], 0.0, 1.0)
        _a = jax.random.uniform(jax.random.fold_in(_gk, 2), (8192, 8192)) < _pij
        _af = _a.astype(jnp.float32)
        _af = _af * jax.random.uniform(jax.random.fold_in(_gk, 3), (8192, 8192), jnp.float32, 0.05, 0.999999)
        adj = _af
        return (x, adj)
    x, adj = _rec_inputs()

    def _L0_gnn_setup():
        import jax, jax.numpy as jnp
        import numpy as np
        N = 3072
        HID = 128
        T = 350
        DENSITY = 0.05
        key = jax.random.key(seed)
        k1, k2, k3, k4, k5, k6 = jax.random.split(key, 6)
        h = jax.random.normal(k1, (N, HID), dtype=jnp.float32)
        a = jax.random.uniform(k2, (N, N), dtype=jnp.float32)
        mask = jax.random.uniform(k3, (N, N)) < DENSITY
        adj = jnp.where(mask, a, 0.0)
        simlar = jax.random.normal(k4, (N, N), dtype=jnp.float32)
        s = 1.0 / np.sqrt(HID)
        W_proj = jax.random.uniform(k5, (HID, HID), minval=-s, maxval=s, dtype=jnp.float32)
        b_proj = jnp.zeros((HID,), dtype=jnp.float32)
        W_gcn = jax.random.uniform(k6, (HID, HID), minval=-s, maxval=s, dtype=jnp.float32)
        b_gcn = jnp.zeros((HID,), dtype=jnp.float32)
        return {'h': h, 'adj': adj, 'simlar': simlar, 'W_proj': W_proj, 'b_proj': b_proj, 'W_gcn': W_gcn, 'b_gcn': b_gcn}
    _L0_gnn_all = _L0_gnn_setup()
    _L0_gnn_in = {k: v for k, v in _L0_gnn_all.items() if k in ('W_proj', 'b_proj', 'W_gcn', 'b_gcn')}
    del _L0_gnn_all
    return {'x': x, 'adj': adj, 'L0_gnn_W_proj': _L0_gnn_in['W_proj'], 'L0_gnn_b_proj': _L0_gnn_in['b_proj'], 'L0_gnn_W_gcn': _L0_gnn_in['W_gcn'], 'L0_gnn_b_gcn': _L0_gnn_in['b_gcn']}

def reference(x, adj, L0_gnn_W_proj, L0_gnn_b_proj, L0_gnn_W_gcn, L0_gnn_b_gcn):
    import jax
    import jax.numpy as jnp

    def _L0_gnn_ref(h, adj, simlar, W_proj, b_proj, W_gcn, b_gcn):
        import jax, jax.numpy as jnp
        import numpy as np
        N = 3072
        HID = 128
        T = 350
        DENSITY = 0.05
        sim = jnp.tanh(adj * simlar)
        filt = sim * (adj > 0).astype(sim.dtype)
        vals, idx = jax.lax.top_k(filt, T)
        nnz = jnp.sum(filt != 0, axis=1)
        keep = jnp.arange(T)[None, :] < nnz[:, None]
        rows = jnp.arange(filt.shape[0])[:, None]
        new_adj = jnp.zeros_like(filt).at[rows, idx].set(jnp.where(keep, vals, 0.0))
        h2 = jnp.tanh(h @ W_proj + b_proj)
        feat = jax.nn.relu(new_adj @ (h2 @ W_gcn) + b_gcn)
        return feat
    x = _layernorm(x + _L0_gnn_ref(x, adj, adj, L0_gnn_W_proj, L0_gnn_b_proj, L0_gnn_W_gcn, L0_gnn_b_gcn), axis=-1)
    return x

_drawn_inputs = setup_inputs


def setup_inputs(seed=0):
    import zlib

    import numpy as np

    out = dict(_drawn_inputs(seed))
    spreads = {'L0_gnn_b_proj': (0.0, 0.1), 'L0_gnn_b_gcn': (0.0, 0.1)}
    factors = {}
    for name, (base, spread) in spreads.items():
        noise = np.random.default_rng([zlib.crc32(name.encode()), seed]).standard_normal(out[name].shape)
        drawn = base * np.exp(spread * noise) if base else spread * noise
        out[name] = jnp.asarray(drawn.astype(out[name].dtype))
    for name, factor in factors.items():
        out[name] = (out[name] * factor).astype(out[name].dtype)
    return out
```

```python
from contextlib import ExitStack

import concourse.bass as bass
import concourse.mybir as mybir
from concourse.alu_op_type import AluOpType as ALU

F32 = mybir.dt.float32
BF16 = mybir.dt.bfloat16
I32 = mybir.dt.int32
ACT = mybir.ActivationFunctionType
AX = mybir.AxisListType

TOP = 350
EPS = 1e-5
D = 128
GROUP = 512
TILES = GROUP // D
CHUNK = 2048
P_COLS = 384
D_COLS = CHUNK - P_COLS
QUARTER = D_COLS // 4
P_BLOCKS = P_COLS // D
D_BLOCKS = D_COLS // D
BLOCKS = P_BLOCKS + D_BLOCKS
P_RING, D_RING, T_RING, F_RING, U_RING = 4, 2, 2, 2, 2
STEP_BITS = 30


def build(nc, x, adj, w_proj, b_proj, w_gcn, b_gcn, eye, same_row, out):
    N = x.shape[0]
    GROUPS = N // GROUP
    PAIRS = GROUPS // 2
    CHUNKS = N // CHUNK
    PAIR_CHUNKS = 2 * CHUNKS
    ROW_TILES = N // D
    assert PAIR_CHUNKS % P_RING == 0 and PAIRS >= 2

    ctx = ExitStack()
    with ctx:
        def sb(name, shape, dt=F32):
            return ctx.enter_context(nc.sbuf_tensor(name, shape, dt))

        def sem(name):
            return ctx.enter_context(nc.semaphore(name))

        p_tiles = sb("p_tiles", [D, P_RING, TILES * P_COLS])
        dt_tiles = sb("dt_tiles", [D, D_RING + T_RING, D_BLOCKS * GROUP])
        d_tiles = dt_tiles[:, 0:D_RING, :]
        t_tiles = dt_tiles[:, D_RING:, :]
        f_tiles = sb("f_tiles", [D, F_RING, P_BLOCKS * GROUP])
        g_sb = sb("g_sb", [D, CHUNKS, BLOCKS, D])
        junk = sb("junk", [D, max(16 * QUARTER, TILES * P_COLS)], BF16)
        x_sb = sb("x_sb", [D, 2, GROUP])
        feat = sb("feat", [D, GROUP])
        y_sb = sb("y_sb", [D, 2, GROUP])
        o_sb = sb("o_sb", [D, 2, GROUP])
        eye_sb = sb("eye_sb", [D, D])
        same_sb = sb("same_sb", [D, D])
        wp_sb = sb("wp_sb", [D, D])
        wg_sb = sb("wg_sb", [D, D])
        bp_sb = sb("bp_sb", [D, 1])
        bg_sb = sb("bg_sb", [D, 1])
        stats = sb("stats", [D, TILES, 6])
        mean = sb("mean", [D, 2, TILES])
        diff = sb("diff", [D, TILES])
        m2 = sb("m2", [D, TILES])
        var_eps = sb("var_eps", [D, 2, TILES])
        centred = sb("centred", [D, GROUP])
        rstd = sb("rstd", [D, TILES])
        minus_half = sb("minus_half", [D, TILES])
        p_count = sb("p_count", [D, GROUPS * CHUNKS])
        d_count = sb("d_count", [D, GROUPS * CHUNKS])
        bound = sb("bound", [D, GROUPS * CHUNKS])
        bound_group = sb("bound_group", [D, GROUPS])
        bound_max = sb("bound_max", [D, 1])
        bound_all = sb("bound_all", [1, 1])
        over_i = sb("over_i", [1, 1], I32)

        x_all = g_sb
        h2_t = t_tiles[:, :, :].rearrange("p s n -> p (s n)")[:, 0:N]
        x_t = f_tiles

        acc = ctx.enter_context(nc.psum_tensor("acc", [D, 2, GROUP], F32))
        tp = ctx.enter_context(nc.psum_tensor("tp", [D, U_RING, P_BLOCKS, GROUP], F32))
        tp_bank = tp[:, :, :, :].rearrange("p s u n -> p (s u) n")

        consts_loaded = sem("consts_loaded")
        x_chunk_loaded = [sem(f"x_chunk_loaded{c}") for c in range(CHUNKS)]
        xt_ready = sem("xt_ready")
        xt_copied = sem("xt_copied")
        pre_ready = sem("pre_ready")
        h2_ready = sem("h2_ready")
        g_ready = sem("g_ready")
        g_copied = sem("g_copied")
        half_set = sem("half_set")
        p_loaded = [sem(f"p_loaded{s}") for s in range(P_RING)]
        d_loaded = [sem(f"d_loaded{s}") for s in range(D_RING)]
        x_loaded = [sem(f"x_loaded{s}") for s in range(2)]
        p_squared = sem("p_squared")
        d_squared = sem("d_squared")
        d_turned = sem("d_turned")
        d_filtered = sem("d_filtered")
        p_counted = sem("p_counted")
        d_counted = sem("d_counted")
        p_turned = sem("p_turned")
        p_filtered = sem("p_filtered")
        chunk_used = sem("chunk_used")
        feat_ready = sem("feat_ready")
        feat_turned = sem("feat_turned")
        y_ready = sem("y_ready")
        stats_ready = sem("stats_ready")
        mv_ready = sem("mv_ready")
        norm_step = sem("norm_step")
        o_ready = sem("o_ready")
        o_stored = [sem(f"o_stored{s}") for s in range(2)]
        bound_mm = sem("bound_mm")
        bound_step = sem("bound_step")
        bound_turned = sem("bound_turned")
        flag_ready = sem("flag_ready")
        e_loaded = sem("e_loaded")
        e_squared = sem("e_squared")
        e_filtered = sem("e_filtered")
        e_step = sem("e_step")
        e_kept = sem("e_kept")
        e_turned = sem("e_turned")
        e_copied = sem("e_copied")
        e_acc = sem("e_acc")
        e_y = sem("e_y")
        e_mv = sem("e_mv")
        e_pool = sem("e_pool")
        e_out = sem("e_out")
        e_stored = sem("e_stored")

        block = ctx.enter_context(nc.Block())

        adj_rows = adj.rearrange("(g t p) n -> g p t n", p=D, t=TILES)
        adj_strips = adj.rearrange("(g i c) n -> g c i n", c=32, i=16)
        x_rows = x.rearrange("(g t p) d -> g p t d", p=D, t=TILES)
        out_rows = out.rearrange("(g t p) d -> g p t d", p=D, t=TILES)

        flat = dt_tiles[:, :, :].rearrange("p s n -> p (s n)")
        e_a, e_f, e_b = (flat[:, n * N:(n + 1) * N] for n in range(3))

        EXACT_STEPS = 2 + 6 * STEP_BITS + 11
        thr_i = sb("thr_i", [D, 1], I32)
        cand_i = sb("cand_i", [D, 1], I32)
        bit_i = sb("bit_i", [D, 1], I32)
        ok_i = sb("ok_i", [D, 1], I32)
        cnt = sb("cnt", [D, 1])
        need = sb("need", [D, 1])

        def exact_rows(dve, V, moments):
            with dve.Fori(0, ROW_TILES) as t:
                base = t * EXACT_STEPS
                thr_f, cand_f = thr_i[:, :].bitcast(F32), cand_i[:, :].bitcast(F32)
                dve.wait_ge(e_loaded, 48 * t + 48)
                V.scalar_tensor_tensor(e_b, e_a, 0.0, e_a, ALU.max, ALU.mult).then_inc(e_squared, 1)
                dve.wait_ge(e_filtered, t + 1)
                V.memset(thr_i[:, :], 0).then_inc(e_step, 1)
                V.memset(bit_i[:, :], 1 << (STEP_BITS - 1)).then_inc(e_step, 1)
                with dve.Fori(0, STEP_BITS) as b:
                    at = base + 2 + 6 * b
                    dve.wait_ge(e_step, at)
                    V.tensor_tensor(cand_i[:, :], thr_i[:, :], bit_i[:, :], ALU.bitwise_or).then_inc(e_step, 1)
                    dve.wait_ge(e_step, at + 1)
                    V.tensor_scalar(e_f, e_a, cand_f, None, ALU.is_ge, ALU.add, accum_out=cnt[:, :]).then_inc(e_step, 1)
                    dve.wait_ge(e_step, at + 2)
                    V.tensor_scalar(ok_i[:, :], cnt[:, :], float(TOP), -1.0, ALU.is_ge, ALU.mult).then_inc(e_step, 1)
                    dve.wait_ge(e_step, at + 3)
                    V.tensor_tensor(ok_i[:, :], ok_i[:, :], bit_i[:, :], ALU.bitwise_and).then_inc(e_step, 1)
                    dve.wait_ge(e_step, at + 4)
                    V.tensor_tensor(thr_i[:, :], thr_i[:, :], ok_i[:, :], ALU.bitwise_or).then_inc(e_step, 1)
                    V.tensor_single_scalar(bit_i[:, :], bit_i[:, :], 1, ALU.logical_shift_right).then_inc(e_step, 1)
                at = base + 2 + 6 * STEP_BITS
                dve.wait_ge(e_step, at)
                V.tensor_scalar(e_f, e_a, thr_f, None, ALU.is_gt, ALU.add, accum_out=cnt[:, :]).then_inc(e_step, 1)
                dve.wait_ge(e_step, at + 1)
                V.tensor_scalar(need[:, :], cnt[:, :], -1.0, float(TOP), ALU.mult, ALU.add).then_inc(e_step, 1)
                V.tensor_scalar(e_f, e_a, thr_f, None, ALU.is_equal).then_inc(e_step, 1)
                dve.wait_ge(e_step, at + 3)
                V.tensor_tensor_scan(e_b, e_f, e_f, 0.0, ALU.add, ALU.max).then_inc(e_step, 1)
                dve.wait_ge(e_step, at + 4)
                V.scalar_tensor_tensor(e_f, e_b, need[:, :], e_f, ALU.is_le, ALU.mult).then_inc(e_step, 1)
                dve.wait_ge(e_step, at + 5)
                V.scalar_tensor_tensor(e_b, e_a, thr_f, e_f, ALU.is_gt, ALU.add).then_inc(e_step, 1)
                dve.wait_ge(e_step, at + 6)
                for c in range(CHUNKS):
                    lo, mid, hi = c * CHUNK, c * CHUNK + P_COLS, (c + 1) * CHUNK
                    V.tensor_tensor(e_f[:, lo:mid], e_a[:, lo:mid], e_b[:, lo:mid], ALU.mult)
                    ins = V.tensor_tensor(e_f[:, mid:hi].rearrange("p (b q r) -> p q b r", q=4, r=32),
                                          e_a[:, mid:hi].rearrange("p (q b r) -> p q b r", q=4, r=32),
                                          e_b[:, mid:hi].rearrange("p (q b r) -> p q b r", q=4, r=32), ALU.mult)
                ins.then_inc(e_kept, 1)
                for n in range(ROW_TILES // 4):
                    m = t * (ROW_TILES // 4) + n
                    dve.wait_ge(e_turned, m + 1)
                    if n == 0:
                        dve.wait_ge(e_kept, t + 1)
                    V.tensor_copy(e_b[:, n * GROUP:(n + 1) * GROUP], tp_bank[:, n % 2, :]).then_inc(e_copied, 1)
                dve.wait_ge(e_acc, t + 1)
                V.tensor_tensor(feat[:, 0:D], acc[:, 0, 0:D], x_sb[:, 1, 0:D], ALU.add).then_inc(e_y, 1)
                dve.wait_ge(e_y, 2 * t + 1)
                V.scalar_tensor_tensor(y_sb[:, 0, 0:D], feat[:, 0:D], 0.0, x_sb[:, 0, 0:D], ALU.max, ALU.add)\
                    .then_inc(e_y, 1)
                dve.wait_ge(e_y, 2 * t + 2)
                V.bn_stats(stats[:, 0, :], y_sb[:, 0, 0:D]).then_inc(e_step, 1)
                moments(e_step, at + 7, 0, 1, e_mv)

        @block.sync
        def _(sp):
            for dst, src in ((eye_sb[:, :], eye), (wp_sb[:, :], w_proj), (wg_sb[:, :], w_gcn), (same_sb[:, :], same_row),
                             (bp_sb[:, :], b_proj.rearrange("(d a) -> d a", a=1)),
                             (bg_sb[:, :], b_gcn.rearrange("(d a) -> d a", a=1))):
                sp.dma_start(dst, src).then_inc(consts_loaded, 16)
            for c in range(CHUNKS):
                sp.dma_start(x_all[:, c, 0:P_BLOCKS, :],
                             x[c * CHUNK:c * CHUNK + P_COLS, :].rearrange("(b p) d -> p b d", p=D))\
                    .then_inc(x_chunk_loaded[c], 16)
                for q in range(4):
                    at = c * CHUNK + P_COLS + q * QUARTER
                    sp.dma_start(x_all[32 * q:32 * q + 32, c, P_BLOCKS:, :],
                                 x[at:at + QUARTER, :].rearrange("(b r) d -> r b d", r=32))\
                        .then_inc(x_chunk_loaded[c], 16)

            def load_pair(i):
                for h in range(2):
                    g = 2 * i + h
                    for c in range(CHUNKS):
                        kk = h * CHUNKS + c
                        k = i * PAIR_CHUNKS + kk
                        sp.wait_ge(p_turned, k + 1)
                        sp.wait_ge(p_counted, k + 1)
                        sp.dma_start(p_tiles[:, kk % P_RING, :].rearrange("p (t n) -> p t n", t=TILES),
                                     adj_rows[bass.ds(g, 1)].rearrange("a p t n -> (a p) t n")[
                                         :, :, c * CHUNK:c * CHUNK + P_COLS]).then_inc(p_loaded[kk % P_RING], 16)
                        sp.wait_ge(d_turned, k + 1)
                        sp.wait_ge(d_counted, k + 1)
                        strips = adj_strips[bass.ds(g, 1)].rearrange("a c i n -> (a c) i n")
                        for q in range(4):
                            at = c * CHUNK + P_COLS + q * QUARTER
                            sp.dma_start(d_tiles[32 * q:32 * q + 32, kk % D_RING, :].rearrange("c (i n) -> c i n", i=16),
                                         strips[:, :, at:at + QUARTER]).then_inc(d_loaded[kk % D_RING], 16)
                        if c == 1:
                            sp.wait_ge(y_ready, g + 1)
                            sp.dma_start(x_sb[:, h, :].rearrange("p (t d) -> p t d", t=TILES),
                                         x_rows[bass.ds(g, 1)].rearrange("a p t d -> (a p) t d")).then_inc(x_loaded[h], 16)

            with sp.Fori(0, PAIRS) as i:
                load_pair(i)

            sp.wait_ge(flag_ready, 1)
            over = sp.value_load(over_i[0:1, 0:1])
            with sp.If(over > 0):
                adj_tiles = adj.rearrange("(t p) n -> t p n", p=D)
                x_tiles = x.rearrange("(t p) d -> t p d", p=D)
                with sp.Fori(0, ROW_TILES) as t:
                    sp.wait_ge(e_out, t + 1)
                    sp.dma_start(e_a, adj_tiles[bass.ds(t, 1)].rearrange("a p n -> (a p) n")).then_inc(e_loaded, 16)
                    sp.dma_start(x_sb[:, 0, 0:D], x_tiles[bass.ds(t, 1)].rearrange("a p n -> (a p) n"))\
                        .then_inc(e_loaded, 16)
                    sp.dma_start(x_sb[:, 1, 0:D], b_gcn.rearrange("(a d) -> a d", a=1).broadcast_to([D, D]))\
                        .then_inc(e_loaded, 16)

        @block.vector
        def _(dve):
            V = nc.vector
            dve.sem_inc(d_turned, D_RING)
            for s in range(N // GROUP):
                dve.wait_ge(xt_ready, s + 1)
                if s >= F_RING:
                    dve.wait_ge(pre_ready, s - F_RING + 1)
                V.tensor_copy(x_t[:, s % F_RING, 0:GROUP], tp_bank[:, s % 3, :]).then_inc(xt_copied, 1)

            def finish(g, slot):
                dve.wait_ge(feat_turned, g + 2)
                dve.wait_ge(x_loaded[slot], 8 * (g - slot) + 16)
                dve.wait_ge(o_ready, g + 1)
                V.tensor_tensor(y_sb[:, slot, :], acc[:, slot, :], x_sb[:, slot, :], ALU.add).then_inc(y_ready, 1)
                dve.wait_ge(y_ready, g + 3)
                dve.wait_ge(mv_ready, g + 1)
                for t in range(TILES):
                    V.bn_stats(stats[:, t, :], y_sb[:, slot, t * D:(t + 1) * D]).then_inc(stats_ready, 1)
                moments(stats_ready, (TILES + 4) * g + TILES, slot, TILES, mv_ready)

            def moments(step, at, slot, tiles, done):
                half = stats[:, 0:tiles, :]
                dve.wait_ge(step, at)
                V.tensor_tensor(mean[:, slot, 0:tiles], half[:, :, 1], half[:, :, 4], ALU.add).then_inc(step, 1)
                V.tensor_tensor(diff[:, 0:tiles], half[:, :, 1], half[:, :, 4], ALU.subtract).then_inc(step, 1)
                V.tensor_tensor(m2[:, 0:tiles], half[:, :, 2], half[:, :, 5], ALU.add).then_inc(step, 1)
                dve.wait_ge(step, at + 3)
                V.tensor_scalar(mean[:, slot, 0:tiles], mean[:, slot, 0:tiles], 0.5, None, ALU.mult)
                V.scalar_tensor_tensor(diff[:, 0:tiles], diff[:, 0:tiles], 0.25, diff[:, 0:tiles], ALU.mult, ALU.mult)
                V.tensor_scalar(m2[:, 0:tiles], m2[:, 0:tiles], 1.0 / D, EPS, ALU.mult, ALU.add).then_inc(step, 1)
                dve.wait_ge(step, at + 4)
                V.tensor_tensor(var_eps[:, slot, 0:tiles], m2[:, 0:tiles], diff[:, 0:tiles], ALU.add).then_inc(done, 1)

            def pair(i, first):
                for h in range(2):
                    g = 2 * i + h
                    for c in range(CHUNKS):
                        kk = h * CHUNKS + c
                        k = i * PAIR_CHUNKS + kk
                        a = d_tiles[:, kk % D_RING, :]
                        dve.wait_ge(d_loaded[kk % D_RING], i * (64 * PAIR_CHUNKS // D_RING) + 64 * (kk // D_RING + 1))
                        V.scalar_tensor_tensor(a, a, 0.0, a, ALU.max, ALU.mult).then_inc(d_squared, 1)
                        b = p_tiles[:, kk % P_RING, :]
                        dve.wait_ge(p_loaded[kk % P_RING], i * (16 * PAIR_CHUNKS // P_RING) + 16 * (kk // P_RING + 1))
                        V.scalar_tensor_tensor(b, b, 0.0, b, ALU.max, ALU.mult).then_inc(p_squared, 1)
                        if first and kk == 0:
                            dve.wait_ge(g_ready, CHUNKS * BLOCKS // 4)
                        dve.wait_ge(d_squared, k + 1)
                        dve.wait_ge(chunk_used, k + 1)
                        turned = t_tiles[:, kk % T_RING, :].rearrange("p (b i r) -> p i b r", i=16, r=32)
                        V.transpose(turned, a.rearrange("p (i b r) -> p i b r", i=16, r=32)).then_inc(d_turned, 1)
                        if c == CHUNKS - 1 and not (first and h == 0):
                            finish(g - 1, 1 - h)

            dve.sem_inc(y_ready, 2)
            dve.sem_inc(mv_ready, 1)
            pair(0, True)
            with dve.Fori(1, PAIRS) as i:
                pair(i, False)
            finish(GROUPS - 1, 1)

            dve.wait_ge(bound_mm, 1)
            dve.wait_ge(p_counted, P_RING + GROUPS * CHUNKS)
            V.tensor_tensor(bound[:, :], acc[:, 0, 0:GROUPS * CHUNKS], p_count[:, :], ALU.add).then_inc(bound_step, 1)
            dve.wait_ge(bound_step, 1)
            V.tensor_reduce(bound_group[:, :], bound[:, :].rearrange("p (g c) -> p g c", c=CHUNKS), AX.X, ALU.add)\
                .then_inc(bound_step, 1)
            dve.wait_ge(bound_step, 2)
            V.tensor_reduce(bound_max[:, :], bound_group[:, :], AX.X, ALU.max).then_inc(bound_step, 1)
            dve.wait_ge(bound_turned, 1)
            V.tensor_reduce(bound_all[:, :], acc[0:1, 1, 0:D], AX.X, ALU.max).then_inc(bound_step, 1)
            dve.wait_ge(bound_step, 4)
            V.tensor_scalar(over_i[:, :], bound_all[:, :], TOP + 0.5, None, ALU.is_gt).then_inc(flag_ready, 1)

            dve.wait_ge(flag_ready, 1)
            over = dve.value_load(over_i[0:1, 0:1])
            dve.wait_ge(o_ready, 2 + GROUPS)
            with dve.If(over > 0):
                exact_rows(dve, V, moments)

        @block.scalar
        def _(act):
            S = nc.scalar
            act.sem_inc(p_counted, P_RING)
            act.sem_inc(p_filtered, U_RING)
            act.sem_inc(d_counted, D_RING)
            act.wait_ge(consts_loaded, 96)
            for s in range(N // GROUP):
                act.wait_ge(pre_ready, s + 1)
                S.activation(h2_t[:, s * GROUP:(s + 1) * GROUP], tp_bank[:, 3 + s % 3, :], ACT.Tanh, bias=bp_sb[:, :])\
                    .then_inc(h2_ready, 1)
            g_flat = g_sb[:, :, :, :].rearrange("p c b d -> p (c b d)")
            for s in range(CHUNKS * BLOCKS // 4):
                act.wait_ge(g_ready, s + 1)
                S.activation(g_flat[:, s * GROUP:(s + 1) * GROUP], tp_bank[:, s % 6, :], ACT.Copy).then_inc(g_copied, 1)

            def filter_d(k, kk):
                act.wait_ge(d_turned, k + 1 + D_RING)
                t = t_tiles[:, kk % T_RING, :]
                S.activation(t, t, ACT.Tanh).then_inc(d_filtered, 1)

            def filter_p(k, kk):
                act.wait_ge(p_turned, P_RING + k + 1)
                act.wait_ge(chunk_used, k + 1)
                S.activation(f_tiles[:, kk % F_RING, :], tp[:, kk % U_RING, :, :].rearrange("p u n -> p (u n)"), ACT.Tanh)\
                    .then_inc(p_filtered, 1)

            def relu(g, slot):
                act.wait_ge(chunk_used, T_RING + CHUNKS * (g + 1))
                act.wait_ge(feat_turned, g + 1)
                S.activation(feat[:, :], acc[:, slot, :], ACT.Relu, bias=bg_sb[:, :]).then_inc(feat_ready, 1)

            def pair(i, first):
                for h in range(2):
                    g = 2 * i + h
                    for c in range(CHUNKS):
                        kk = h * CHUNKS + c
                        k = i * PAIR_CHUNKS + kk
                        act.wait_ge(p_counted, P_RING + k)
                        act.wait_ge(d_squared, k + 1)
                        S.activation(junk[:, 0:16 * QUARTER], d_tiles[:, kk % D_RING, :], ACT.Sign,
                                     accum_out=d_count[:, bass.ds(k, 1)]).then_inc(d_counted, 1)
                        act.wait_ge(d_counted, D_RING + k + 1)
                        act.wait_ge(p_squared, k + 1)
                        S.activation(junk[:, 0:TILES * P_COLS], p_tiles[:, kk % P_RING, :], ACT.Sign,
                                     accum_out=p_count[:, bass.ds(k, 1)]).then_inc(p_counted, 1)
                        filter_d(k, kk)
                        filter_p(k, kk)
                        if c == 1 and not (first and h == 0):
                            relu(g - 1, 1 - h)

            pair(0, True)
            with act.Fori(1, PAIRS) as i:
                pair(i, False)
            relu(GROUPS - 1, 1)

            act.wait_ge(flag_ready, 1)
            over = act.value_load(over_i[0:1, 0:1])
            for s in range(2):
                act.wait_ge(o_stored[s], 16 * PAIRS)
            out_tiles = out.rearrange("(t p) d -> t p d", p=D)
            with act.If(over > 0):
                with act.Fori(0, ROW_TILES) as t:
                    act.wait_ge(e_squared, t + 1)
                    S.activation(e_a, e_b, ACT.Tanh).then_inc(e_filtered, 1)
                    act.wait_ge(e_out, t + 2)
                    act.dma_start(out_tiles[bass.ds(t, 1)].rearrange("a p n -> (a p) n"), o_sb[:, 0, 0:D])\
                        .then_inc(e_stored, 16)
                    act.wait_ge(e_stored, 16 * t + 16)

        @block.tensor
        def _(pe):
            T = nc.tensor
            pe.sem_inc(p_turned, P_RING)
            pe.sem_inc(chunk_used, T_RING)
            pe.sem_inc(feat_turned, 1)
            pe.wait_ge(consts_loaded, 96)

            def project(s):
                pe.wait_ge(xt_copied, s + 1)
                if s >= 3:
                    pe.wait_ge(h2_ready, s - 2)
                T.matmul(tp_bank[:, 3 + s % 3, :], wp_sb[:, :], x_t[:, s % F_RING, 0:GROUP], start=True, stop=True)\
                    .then_inc(pre_ready, 1)

            for s in range(N // GROUP):
                if s * TILES % BLOCKS == 0:
                    pe.wait_ge(x_chunk_loaded[s * TILES // BLOCKS], 80)
                if s >= 3:
                    pe.wait_ge(xt_copied, s - 2)
                for t in range(TILES):
                    ins = T.transpose(tp_bank[:, s % 3, t * D:(t + 1) * D], x_all[:, (s * TILES + t) // BLOCKS, (s * TILES + t) % BLOCKS, :], eye_sb[:, :])
                ins.then_inc(xt_ready, 1)
                if s >= 1:
                    project(s - 1)
            project(N // GROUP - 1)
            for s in range(CHUNKS * BLOCKS // 4):
                if s == 0:
                    pe.wait_ge(h2_ready, N // GROUP)
                if s >= 6:
                    pe.wait_ge(g_copied, s - 5)
                for n in range(4):
                    m = 4 * s + n
                    ins = T.matmul(tp_bank[:, s % 6, n * D:(n + 1) * D], h2_t[:, m * D:(m + 1) * D], wg_sb[:, :],
                                   start=True, stop=True)
                ins.then_inc(g_ready, 1)
            pe.wait_ge(g_copied, CHUNKS * BLOCKS // 4)

            def turn(i, kk):
                pe.wait_ge(p_filtered, i * PAIR_CHUNKS + kk + 1)
                pe.wait_ge(p_squared, i * PAIR_CHUNKS + kk + 1)
                rows = p_tiles[:, kk % P_RING, :].rearrange("p (t n) -> p t n", t=TILES)
                for b in range(P_BLOCKS):
                    for t in range(TILES):
                        ins = T.transpose(tp[:, kk % U_RING, b, t * D:(t + 1) * D], rows[:, t, b * D:(b + 1) * D],
                                          eye_sb[:, :])
                ins.then_inc(p_turned, 1)

            def multiply(i, kk):
                h, c = divmod(kk, CHUNKS)
                if c == 0 and not (isinstance(i, int) and i == 0):
                    pe.wait_ge(y_ready, 2 * i + h + 1)
                pe.wait_ge(d_filtered, i * PAIR_CHUNKS + kk + 1)
                for b in range(D_BLOCKS):
                    T.matmul(acc[:, h, :], g_sb[:, c, P_BLOCKS + b, :], t_tiles[:, kk % T_RING, b * GROUP:(b + 1) * GROUP],
                             start=(c == 0 and b == 0), stop=False)
                pe.wait_ge(p_filtered, U_RING + i * PAIR_CHUNKS + kk + 1)
                for b in range(P_BLOCKS):
                    ins = T.matmul(acc[:, h, :], g_sb[:, c, b, :], f_tiles[:, kk % F_RING, b * GROUP:(b + 1) * GROUP],
                                   start=False, stop=(c == CHUNKS - 1 and b == P_BLOCKS - 1))
                ins.then_inc(chunk_used, 1)

            def turn_back(g, slot):
                pe.wait_ge(feat_ready, g + 1)
                for t in range(TILES):
                    ins = T.transpose(acc[:, slot, t * D:(t + 1) * D], feat[:, t * D:(t + 1) * D], eye_sb[:, :])
                ins.then_inc(feat_turned, 1)

            def pair(i, first):
                for kk in range(PAIR_CHUNKS):
                    h, c = divmod(kk, CHUNKS)
                    turn(i, kk)
                    if c == min(2, CHUNKS - 1) and not (first and h == 0):
                        turn_back(2 * i + h - 1, 1 - h)
                    if kk >= 1:
                        multiply(i, kk - 1)
                    elif not first:
                        multiply(i - 1, PAIR_CHUNKS - 1)

            pair(0, True)
            with pe.Fori(1, PAIRS) as i:
                pair(i, False)
            multiply(PAIRS - 1, PAIR_CHUNKS - 1)
            turn_back(GROUPS - 1, 1)

            pe.wait_ge(d_counted, D_RING + GROUPS * CHUNKS)
            pe.wait_ge(y_ready, 2 + GROUPS)
            T.matmul(acc[:, 0, 0:GROUPS * CHUNKS], same_sb[:, :], d_count[:, :], start=True, stop=True).then_inc(bound_mm, 1)
            pe.wait_ge(bound_step, 3)
            T.transpose(acc[0:1, 1, 0:D], bound_max[:, :], eye_sb[:, :]).then_inc(bound_turned, 1)

            pe.wait_ge(flag_ready, 1)
            over = pe.value_load(over_i[0:1, 0:1])
            with pe.If(over > 0):
                with pe.Fori(0, ROW_TILES) as t:
                    pe.wait_ge(e_kept, t + 1)
                    for n in range(ROW_TILES // 4):
                        if n >= 2:
                            pe.wait_ge(e_copied, t * (ROW_TILES // 4) + n - 1)
                        for w in range(4):
                            m = 4 * n + w
                            ins = T.transpose(tp_bank[:, n % 2, w * D:(w + 1) * D], e_f[:, m * D:(m + 1) * D], eye_sb[:, :])
                        ins.then_inc(e_turned, 1)
                    pe.wait_ge(e_copied, (t + 1) * (ROW_TILES // 4))
                    for n in range(ROW_TILES):
                        c, b = divmod(n, BLOCKS)
                        ins = T.matmul(acc[:, 0, 0:D], e_b[:, n * D:(n + 1) * D], g_sb[:, c, b, :],
                                       start=(n == 0), stop=(n == ROW_TILES - 1))
                    ins.then_inc(e_acc, 1)

        @block.gpsimd
        def _(pool):
            G = nc.gpsimd
            G.memset(minus_half[:, :], -0.5).then_inc(half_set, 1)
            pool.sem_inc(o_ready, 2)
            pool.wait_ge(half_set, 1)

            def normalise(g, slot, first):
                y = y_sb[:, slot, :].rearrange("p (t d) -> p t d", t=TILES)
                z = centred[:, :].rearrange("p (t d) -> p t d", t=TILES)
                pool.wait_ge(mv_ready, g + 2)
                G.tensor_tensor(z, y, mean[:, slot, :].unsqueeze(2).broadcast_to([D, TILES, D]), ALU.subtract)\
                    .then_inc(norm_step, 1)
                G.tensor_tensor(rstd[:, :], var_eps[:, slot, :], minus_half[:, :], ALU.pow).then_inc(norm_step, 1)
                if not first:
                    pool.wait_ge(o_stored[slot], 8 * (g - slot))
                pool.wait_ge(norm_step, 2 * g + 2)
                G.tensor_tensor(o_sb[:, slot, :].rearrange("p (t d) -> p t d", t=TILES), z,
                                rstd[:, :].unsqueeze(2).broadcast_to([D, TILES, D]), ALU.mult).then_inc(o_ready, 1)
                pool.wait_ge(o_ready, g + 3)
                pool.dma_start(out_rows[bass.ds(g, 1)].rearrange("a p t d -> (a p) t d"),
                               o_sb[:, slot, :].rearrange("p (t d) -> p t d", t=TILES)).then_inc(o_stored[slot], 16)

            for h in range(2):
                normalise(h, h, True)
            with pool.Fori(1, PAIRS) as i:
                for h in range(2):
                    normalise(2 * i + h, h, False)
            for s in range(2):
                pool.wait_ge(o_stored[s], 16 * PAIRS)

            pool.wait_ge(flag_ready, 1)
            over = pool.value_load(over_i[0:1, 0:1])
            with pool.If(over > 0):
                pool.sem_inc(e_out, 1)
                with pool.Fori(0, ROW_TILES) as t:
                    pool.wait_ge(e_mv, t + 1)
                    G.tensor_tensor(centred[:, 0:D], y_sb[:, 0, 0:D], mean[:, 0, 0:1].broadcast_to([D, D]),
                                    ALU.subtract).then_inc(e_pool, 1)
                    G.tensor_tensor(rstd[:, 0:1], var_eps[:, 0, 0:1], minus_half[:, 0:1], ALU.pow).then_inc(e_pool, 1)
                    pool.wait_ge(e_pool, 2 * t + 2)
                    G.tensor_tensor(o_sb[:, 0, 0:D], centred[:, 0:D], rstd[:, 0:1].broadcast_to([D, D]), ALU.mult)\
                        .then_inc(e_out, 1)


_INS = ["x", "adj", "L0_gnn_W_proj", "L0_gnn_b_proj", "L0_gnn_W_gcn", "L0_gnn_b_gcn"]


def kernel(**inputs):
    import numpy as np
    import concourse.bacc as bacc
    from concourse.bass_utils import run_bass_kernel_spmd

    nc = bacc.Bacc("TRN2", target_bir_lowering=False, num_devices=1)
    row = np.arange(D)
    arrays = {f"in_{name}": np.ascontiguousarray(inputs[name]) for name in _INS}
    arrays["in_eye"] = np.eye(D, dtype=np.float32)
    arrays["in_same_row"] = (row[:, None] % 32 == row[None, :] % 32).astype(np.float32)
    args = [nc.dram_tensor(name, a.shape, mybir.dt.from_np(a.dtype), kind="ExternalInput").ap() for name, a in arrays.items()]
    out = nc.dram_tensor("out_dram", arrays["in_x"].shape, F32, kind="ExternalOutput").ap()
    build(nc, *args, out)
    return run_bass_kernel_spmd(nc, [arrays], core_ids=[0]).results[0]["out_dram"]
```

```python
from contextlib import ExitStack

import concourse.bass as bass
import concourse.mybir as mybir
from concourse.alu_op_type import AluOpType as ALU

F32 = mybir.dt.float32
BF16 = mybir.dt.bfloat16
I32 = mybir.dt.int32
ACT = mybir.ActivationFunctionType
AX = mybir.AxisListType

TOP = 350
EPS = 1e-5
D = 128
GROUP = 512
TILES = GROUP // D
CHUNK = 1024
QUARTER = CHUNK // 4
BLOCKS = CHUNK // D
STRIPS = GROUP // 32
A_RING = 4
T_RING = 4
FOLD_ROWS = 4
FOLDS = 128 // FOLD_ROWS
ON_VECTOR = 4
STEP_BITS = 30


def build(nc, x, adj, w_proj, b_proj, w_gcn, b_gcn, eye, same_row, same_fold, fold, out):
    N = x.shape[0]
    GROUPS = N // GROUP
    PAIRS = GROUPS // 2
    CHUNKS = N // CHUNK
    PAIR_CHUNKS = 2 * CHUNKS
    ROW_TILES = N // D
    COUNTS = (GROUPS - 1) * CHUNKS // 2
    assert CHUNKS % 4 == 0 and PAIRS >= 2

    ctx = ExitStack()
    with ctx:
        def sb(name, shape, dt=F32):
            return ctx.enter_context(nc.sbuf_tensor(name, shape, dt))

        def sem(name):
            return ctx.enter_context(nc.semaphore(name))

        a_tiles = sb("a_tiles", [D, A_RING, STRIPS * QUARTER])
        t_tiles = sb("t_tiles", [D, T_RING, BLOCKS * GROUP])
        g_sb = sb("g_sb", [D, CHUNKS, BLOCKS, D])
        junk = sb("junk", [D, TILES, STRIPS * QUARTER // TILES], BF16)
        x_sb = sb("x_sb", [D, 2, GROUP])
        feat = sb("feat", [D, GROUP])
        y_sb = sb("y_sb", [D, 2, GROUP])
        o_sb = sb("o_sb", [D, 2, GROUP])
        eye_sb = sb("eye_sb", [D, D])
        same_row_sb = sb("same_row_sb", [D, D])
        same_fold_sb = sb("same_fold_sb", [D, D])
        fold_sb = sb("fold_sb", [D, FOLDS])
        fold_bf = sb("fold_bf", [D, FOLDS], BF16)
        wp_sb = sb("wp_sb", [D, D])
        wg_sb = sb("wg_sb", [D, D])
        bp_sb = sb("bp_sb", [D, 1])
        bg_sb = sb("bg_sb", [D, 1])
        stats = sb("stats", [D, TILES, 6])
        mean = sb("mean", [D, 2, TILES])
        diff = sb("diff", [D, TILES])
        m2 = sb("m2", [D, TILES])
        var_eps = sb("var_eps", [D, 2, TILES])
        centred = sb("centred", [D, GROUP])
        rstd = sb("rstd", [D, TILES])
        minus_half = sb("minus_half", [D, TILES])
        a_count = sb("a_count", [D, CHUNKS, TILES])
        f_count = sb("f_count", [D, COUNTS])
        bound = sb("bound", [D, TILES + GROUPS - 1])
        bound_max = sb("bound_max", [D, 1])
        bound_all = sb("bound_all", [1, 1])
        over_i = sb("over_i", [1, 1], I32)

        x_all = g_sb
        h2_t = t_tiles[:, 2:4, :].rearrange("p s n -> p (s n)")[:, 0:N]
        x_t = t_tiles[:, 1, :].rearrange("p (s n) -> p s n", n=GROUP)
        X_RING = BLOCKS

        acc = ctx.enter_context(nc.psum_tensor("acc", [D, 2, GROUP], F32))
        work = ctx.enter_context(nc.psum_tensor("work", [D, 6, GROUP], F32))

        consts_loaded = sem("consts_loaded")
        x_chunk_loaded = [sem(f"x_chunk_loaded{c}") for c in range(CHUNKS)]
        xt_ready = sem("xt_ready")
        xt_copied = sem("xt_copied")
        pre_ready = sem("pre_ready")
        h2_ready = sem("h2_ready")
        g_ready = sem("g_ready")
        g_copied = sem("g_copied")
        half_set = sem("half_set")
        a_loaded = [sem(f"a_loaded{s}") for s in range(A_RING)]
        x_loaded = [sem(f"x_loaded{s}") for s in range(2)]
        cut_ready = sem("cut_ready")
        squared_v = sem("squared_v")
        squared_s = sem("squared_s")
        turned = sem("turned")
        filtered = sem("filtered")
        used = sem("used")
        a_counted = sem("a_counted")
        folded = sem("folded")
        f_counted = sem("f_counted")
        fold_ready = sem("fold_ready")
        feat_ready = sem("feat_ready")
        feat_turned = sem("feat_turned")
        y_ready = sem("y_ready")
        stats_ready = sem("stats_ready")
        mv_ready = sem("mv_ready")
        norm_step = sem("norm_step")
        o_ready = sem("o_ready")
        o_stored = [sem(f"o_stored{s}") for s in range(2)]
        bound_mm = sem("bound_mm")
        bound_step = sem("bound_step")
        bound_turned = sem("bound_turned")
        flag_ready = sem("flag_ready")
        e_loaded = sem("e_loaded")
        e_squared = sem("e_squared")
        e_filtered = sem("e_filtered")
        e_step = sem("e_step")
        e_kept = sem("e_kept")
        e_turned = sem("e_turned")
        e_copied = sem("e_copied")
        e_acc = sem("e_acc")
        e_y = sem("e_y")
        e_mv = sem("e_mv")
        e_pool = sem("e_pool")
        e_out = sem("e_out")
        e_stored = sem("e_stored")

        block = ctx.enter_context(nc.Block())

        adj_flat = adj.rearrange("r n -> (r n)")
        x_flat = x.rearrange("r d -> (r d)")
        out_rows = out.rearrange("(g t p) d -> g p t d", p=D, t=TILES)

        e_a, e_b = (a_tiles[:, 2 * n:2 * n + 2, :].rearrange("p s n -> p (s n)")[:, 0:N] for n in range(2))
        e_f = t_tiles[:, 0:2, :].rearrange("p s n -> p (s n)")[:, 0:N]

        def square_on_vector(i, kk):
            return (isinstance(i, int) and i == 0 and kk < CHUNKS) or kk % ON_VECTOR == 0

        def wait_squared(engine, i, kk):
            later = ON_VECTOR - 1
            if isinstance(i, int) and i == 0:
                if kk < CHUNKS:
                    engine.wait_ge(squared_v, kk + 1)
                elif kk % ON_VECTOR == 0:
                    engine.wait_ge(squared_v, CHUNKS + (kk - CHUNKS) // ON_VECTOR + 1)
                else:
                    engine.wait_ge(squared_s, (kk - CHUNKS) // ON_VECTOR * later + kk % ON_VECTOR)
            elif kk % ON_VECTOR == 0:
                engine.wait_ge(squared_v, CHUNKS - CHUNKS // ON_VECTOR + i * (PAIR_CHUNKS // ON_VECTOR) + kk // ON_VECTOR + 1)
            else:
                engine.wait_ge(squared_s, (i * (PAIR_CHUNKS // ON_VECTOR) - CHUNKS // ON_VECTOR + kk // ON_VECTOR) * later
                               + kk % ON_VECTOR)

        EXACT_STEPS = 2 + 6 * STEP_BITS + 11
        thr_i = sb("thr_i", [D, 1], I32)
        cand_i = sb("cand_i", [D, 1], I32)
        bit_i = sb("bit_i", [D, 1], I32)
        ok_i = sb("ok_i", [D, 1], I32)
        cnt = sb("cnt", [D, 1])
        need = sb("need", [D, 1])

        def exact_rows(dve, V, moments):
            with dve.Fori(0, ROW_TILES) as t:
                base = t * EXACT_STEPS
                thr_f, cand_f = thr_i[:, :].bitcast(F32), cand_i[:, :].bitcast(F32)
                dve.wait_ge(e_loaded, 48 * t + 48)
                V.scalar_tensor_tensor(e_b, e_a, 0.0, e_a, ALU.max, ALU.mult).then_inc(e_squared, 1)
                dve.wait_ge(e_filtered, t + 1)
                V.memset(thr_i[:, :], 0).then_inc(e_step, 1)
                V.memset(bit_i[:, :], 1 << (STEP_BITS - 1)).then_inc(e_step, 1)
                with dve.Fori(0, STEP_BITS) as b:
                    at = base + 2 + 6 * b
                    dve.wait_ge(e_step, at)
                    V.tensor_tensor(cand_i[:, :], thr_i[:, :], bit_i[:, :], ALU.bitwise_or).then_inc(e_step, 1)
                    dve.wait_ge(e_step, at + 1)
                    V.tensor_scalar(e_f, e_a, cand_f, None, ALU.is_ge, ALU.add, accum_out=cnt[:, :]).then_inc(e_step, 1)
                    dve.wait_ge(e_step, at + 2)
                    V.tensor_scalar(ok_i[:, :], cnt[:, :], float(TOP), -1.0, ALU.is_ge, ALU.mult).then_inc(e_step, 1)
                    dve.wait_ge(e_step, at + 3)
                    V.tensor_tensor(ok_i[:, :], ok_i[:, :], bit_i[:, :], ALU.bitwise_and).then_inc(e_step, 1)
                    dve.wait_ge(e_step, at + 4)
                    V.tensor_tensor(thr_i[:, :], thr_i[:, :], ok_i[:, :], ALU.bitwise_or).then_inc(e_step, 1)
                    V.tensor_single_scalar(bit_i[:, :], bit_i[:, :], 1, ALU.logical_shift_right).then_inc(e_step, 1)
                at = base + 2 + 6 * STEP_BITS
                dve.wait_ge(e_step, at)
                V.tensor_scalar(e_f, e_a, thr_f, None, ALU.is_gt, ALU.add, accum_out=cnt[:, :]).then_inc(e_step, 1)
                dve.wait_ge(e_step, at + 1)
                V.tensor_scalar(need[:, :], cnt[:, :], -1.0, float(TOP), ALU.mult, ALU.add).then_inc(e_step, 1)
                V.tensor_scalar(e_f, e_a, thr_f, None, ALU.is_equal).then_inc(e_step, 1)
                dve.wait_ge(e_step, at + 3)
                V.tensor_tensor_scan(e_b, e_f, e_f, 0.0, ALU.add, ALU.max).then_inc(e_step, 1)
                dve.wait_ge(e_step, at + 4)
                V.scalar_tensor_tensor(e_f, e_b, need[:, :], e_f, ALU.is_le, ALU.mult).then_inc(e_step, 1)
                dve.wait_ge(e_step, at + 5)
                V.scalar_tensor_tensor(e_b, e_a, thr_f, e_f, ALU.is_gt, ALU.add).then_inc(e_step, 1)
                dve.wait_ge(e_step, at + 6)
                for c in range(CHUNKS):
                    lo, hi = c * CHUNK, (c + 1) * CHUNK
                    ins = V.tensor_tensor(e_f[:, lo:hi].rearrange("p (b q r) -> p q b r", q=4, r=32),
                                          e_a[:, lo:hi].rearrange("p (q b r) -> p q b r", q=4, r=32),
                                          e_b[:, lo:hi].rearrange("p (q b r) -> p q b r", q=4, r=32), ALU.mult)
                ins.then_inc(e_kept, 1)
                for n in range(ROW_TILES // 4):
                    m = t * (ROW_TILES // 4) + n
                    dve.wait_ge(e_turned, m + 1)
                    if n == 0:
                        dve.wait_ge(e_kept, t + 1)
                    V.tensor_copy(e_b[:, n * GROUP:(n + 1) * GROUP], work[:, n % 2, :]).then_inc(e_copied, 1)
                dve.wait_ge(e_acc, t + 1)
                V.tensor_tensor(feat[:, 0:D], acc[:, 0, 0:D], x_sb[:, 1, 0:D], ALU.add).then_inc(e_y, 1)
                dve.wait_ge(e_y, 2 * t + 1)
                V.scalar_tensor_tensor(y_sb[:, 0, 0:D], feat[:, 0:D], 0.0, x_sb[:, 0, 0:D], ALU.max, ALU.add)\
                    .then_inc(e_y, 1)
                dve.wait_ge(e_y, 2 * t + 2)
                V.bn_stats(stats[:, 0, :], y_sb[:, 0, 0:D]).then_inc(e_step, 1)
                moments(e_step, at + 7, 0, 1, e_mv)

        @block.sync
        def _(sp):
            for dst, src in ((eye_sb[:, :], eye), (wp_sb[:, :], w_proj), (wg_sb[:, :], w_gcn),
                             (bp_sb[:, :], b_proj.rearrange("(d a) -> d a", a=1)),
                             (bg_sb[:, :], b_gcn.rearrange("(d a) -> d a", a=1)),
                             (same_row_sb[:, :], same_row), (same_fold_sb[:, :], same_fold), (fold_sb[:, :], fold)):
                sp.dma_start(dst, src).then_inc(consts_loaded, 16)
            for c in range(CHUNKS):
                for q in range(4):
                    at = c * CHUNK + q * QUARTER
                    sp.dma_start(x_all[32 * q:32 * q + 32, c, :, :],
                                 x[at:at + QUARTER, :].rearrange("(b r) d -> r b d", r=32))\
                        .then_inc(x_chunk_loaded[c], 16)

            def load_pair(i, first):
                for h in range(2):
                    g = 2 * i + h
                    adj_at, x_at = (g * (GROUP * w) if first else sp.snap(g * (GROUP * w)) for w in (N, D))
                    strips = adj_flat[bass.ds(adj_at, GROUP * N)].rearrange("(i c n) -> c i n", c=32, n=N)
                    for c in range(CHUNKS):
                        kk = h * CHUNKS + c
                        k = i * PAIR_CHUNKS + kk
                        if not (first and kk < A_RING):
                            if first and kk - A_RING < CHUNKS:
                                sp.wait_ge(a_counted, kk - A_RING + 1)
                            else:
                                sp.wait_ge(folded, k - (A_RING - 1))
                            sp.wait_ge(turned, k - (A_RING - 1))
                        for q in range(4):
                            at = c * CHUNK + q * QUARTER
                            sp.dma_start(a_tiles[32 * q:32 * q + 32, kk % A_RING, :].rearrange("c (i n) -> c i n", i=STRIPS),
                                         strips[:, :, at:at + QUARTER]).then_inc(a_loaded[kk % A_RING], 16)
                        if c == CHUNKS // 4:
                            sp.wait_ge(y_ready, g + 1)
                            sp.dma_start(x_sb[:, h, :].rearrange("p (t d) -> p t d", t=TILES),
                                         x_flat[bass.ds(x_at, GROUP * D)].rearrange("(t p d) -> p t d", p=D, d=D))\
                                .then_inc(x_loaded[h], 16)

            load_pair(0, True)
            with sp.Fori(1, PAIRS) as i:
                load_pair(i, False)

            sp.wait_ge(flag_ready, 1)
            over = sp.value_load(over_i[0:1, 0:1])
            with sp.If(over > 0):
                adj_tiles = adj.rearrange("(t p) n -> t p n", p=D)
                x_tiles = x.rearrange("(t p) d -> t p d", p=D)
                with sp.Fori(0, ROW_TILES) as t:
                    sp.wait_ge(e_out, t + 1)
                    sp.dma_start(e_a, adj_tiles[bass.ds(t, 1)].rearrange("a p n -> (a p) n")).then_inc(e_loaded, 16)
                    sp.dma_start(x_sb[:, 0, 0:D], x_tiles[bass.ds(t, 1)].rearrange("a p n -> (a p) n"))\
                        .then_inc(e_loaded, 16)
                    sp.dma_start(x_sb[:, 1, 0:D], b_gcn.rearrange("(a d) -> a d", a=1).broadcast_to([D, D]))\
                        .then_inc(e_loaded, 16)

        @block.vector
        def _(dve):
            V = nc.vector
            dve.wait_ge(consts_loaded, 128)
            V.tensor_copy(fold_bf[:, :], fold_sb[:, :]).then_inc(fold_ready, 1)
            for s in range(N // GROUP):
                dve.wait_ge(xt_ready, s + 1)
                if s >= X_RING:
                    dve.wait_ge(pre_ready, s - X_RING + 1)
                V.tensor_copy(x_t[:, s % X_RING, :], work[:, s % 3, :]).then_inc(xt_copied, 1)

            def finish(g, slot):
                dve.wait_ge(feat_turned, g + 2)
                dve.wait_ge(x_loaded[slot], 8 * (g - slot) + 16)
                dve.wait_ge(o_ready, g + 1)
                V.tensor_tensor(y_sb[:, slot, :], acc[:, slot, :], x_sb[:, slot, :], ALU.add).then_inc(y_ready, 1)
                dve.wait_ge(y_ready, g + 3)
                dve.wait_ge(mv_ready, g + 1)
                for t in range(TILES):
                    V.bn_stats(stats[:, t, :], y_sb[:, slot, t * D:(t + 1) * D]).then_inc(stats_ready, 1)
                moments(stats_ready, (TILES + 4) * g + TILES, slot, TILES, mv_ready)

            def moments(step, at, slot, tiles, done):
                half = stats[:, 0:tiles, :]
                dve.wait_ge(step, at)
                V.tensor_tensor(mean[:, slot, 0:tiles], half[:, :, 1], half[:, :, 4], ALU.add).then_inc(step, 1)
                V.tensor_tensor(diff[:, 0:tiles], half[:, :, 1], half[:, :, 4], ALU.subtract).then_inc(step, 1)
                V.tensor_tensor(m2[:, 0:tiles], half[:, :, 2], half[:, :, 5], ALU.add).then_inc(step, 1)
                dve.wait_ge(step, at + 3)
                V.tensor_scalar(mean[:, slot, 0:tiles], mean[:, slot, 0:tiles], 0.5, None, ALU.mult)
                V.scalar_tensor_tensor(diff[:, 0:tiles], diff[:, 0:tiles], 0.25, diff[:, 0:tiles], ALU.mult, ALU.mult)
                V.tensor_scalar(m2[:, 0:tiles], m2[:, 0:tiles], 1.0 / D, EPS, ALU.mult, ALU.add).then_inc(step, 1)
                dve.wait_ge(step, at + 4)
                V.tensor_tensor(var_eps[:, slot, 0:tiles], m2[:, 0:tiles], diff[:, 0:tiles], ALU.add).then_inc(done, 1)

            def square(i, kk):
                a = a_tiles[:, kk % A_RING, :]
                dve.wait_ge(a_loaded[kk % A_RING], i * (64 * PAIR_CHUNKS // A_RING) + 64 * (kk // A_RING + 1))
                if square_on_vector(i, kk):
                    V.scalar_tensor_tensor(a, a, 0.0, a, ALU.max, ALU.mult).then_inc(squared_v, 1)
                else:
                    V.tensor_scalar(a, a, 0.0, None, ALU.max).then_inc(cut_ready, 1)

            def turn(i, kk):
                if isinstance(i, int) and i == 0 and kk == 1:
                    dve.wait_ge(pre_ready, N // GROUP)
                if isinstance(i, int) and i == 0 and kk == 2:
                    dve.wait_ge(g_ready, CHUNKS * BLOCKS // 4)
                wait_squared(dve, i, kk)
                dve.wait_ge(used, i * PAIR_CHUNKS + kk + 1)
                V.transpose(t_tiles[:, kk % T_RING, :].rearrange("p (b i r) -> p i b r", i=STRIPS, r=32),
                            a_tiles[:, kk % A_RING, :].rearrange("p (i b r) -> p i b r", i=STRIPS, r=32)).then_inc(turned, 1)

            def pair(i, first):
                for kk in range(PAIR_CHUNKS):
                    h, c = divmod(kk, CHUNKS)
                    square(i, kk)
                    if kk >= 1:
                        turn(i, kk - 1)
                    elif not first:
                        turn(i - 1, PAIR_CHUNKS - 1)
                    if c == 3 * CHUNKS // 4 and not (first and h == 0):
                        finish(2 * i + h - 1, 1 - h)

            dve.sem_inc(y_ready, 2)
            dve.sem_inc(mv_ready, 1)
            pair(0, True)
            with dve.Fori(1, PAIRS) as i:
                pair(i, False)
            turn(PAIRS - 1, PAIR_CHUNKS - 1)

            dve.wait_ge(bound_mm, 2)
            V.tensor_reduce(bound[:, 0:TILES], work[:, 4, 0:CHUNKS * TILES].rearrange("p (c t) -> p t c", t=TILES),
                            AX.X, ALU.add).then_inc(bound_step, 1)
            V.tensor_reduce(bound[:, TILES:], work[:, 5, 0:COUNTS].rearrange("p (g c) -> p g c", c=CHUNKS // 2),
                            AX.X, ALU.add).then_inc(bound_step, 1)
            dve.wait_ge(bound_step, 2)
            V.tensor_reduce(bound_max[:, :], bound[:, :], AX.X, ALU.max).then_inc(bound_step, 1)
            finish(GROUPS - 1, 1)
            dve.wait_ge(bound_turned, 1)
            V.tensor_reduce(bound_all[:, :], work[0:1, 0, 0:D], AX.X, ALU.max).then_inc(bound_step, 1)
            dve.wait_ge(bound_step, 4)
            V.tensor_scalar(over_i[:, :], bound_all[:, :], TOP + 0.5, None, ALU.is_gt).then_inc(flag_ready, 1)

            dve.wait_ge(flag_ready, 1)
            over = dve.value_load(over_i[0:1, 0:1])
            dve.wait_ge(o_ready, 2 + GROUPS)
            with dve.If(over > 0):
                exact_rows(dve, V, moments)

        @block.scalar
        def _(act):
            S = nc.scalar
            act.sem_inc(f_counted, 2)
            act.wait_ge(consts_loaded, 128)
            for s in range(N // GROUP):
                act.wait_ge(pre_ready, s + 1)
                S.activation(h2_t[:, s * GROUP:(s + 1) * GROUP], work[:, 3 + s % 3, :], ACT.Tanh, bias=bp_sb[:, :])\
                    .then_inc(h2_ready, 1)
            g_flat = g_sb[:, :, :, :].rearrange("p c b d -> p (c b d)")
            for s in range(CHUNKS * BLOCKS // 4):
                act.wait_ge(g_ready, s + 1)
                S.activation(g_flat[:, s * GROUP:(s + 1) * GROUP], work[:, s % 6, :], ACT.Copy).then_inc(g_copied, 1)

            def square(i, kk):
                if isinstance(i, int) and i == 0:
                    n = (kk - CHUNKS) // ON_VECTOR * (ON_VECTOR - 1) + kk % ON_VECTOR
                else:
                    n = (i * (PAIR_CHUNKS // ON_VECTOR) - CHUNKS // ON_VECTOR + kk // ON_VECTOR) * (ON_VECTOR - 1) + kk % ON_VECTOR
                act.wait_ge(cut_ready, n)
                a = a_tiles[:, kk % A_RING, :]
                S.activation(a, a, ACT.Square).then_inc(squared_s, 1)

            def count_first_group(kk):
                act.wait_ge(squared_v, kk + 1)
                if kk >= 1:
                    act.wait_ge(a_counted, kk)
                rows = a_tiles[:, kk % A_RING, :].rearrange("p (t n) -> p t n", t=TILES)
                for t in range(TILES):
                    ins = S.activation(junk[:, t, :], rows[:, t, :], ACT.Sign, accum_out=a_count[:, kk, t:t + 1])
                ins.then_inc(a_counted, 1)

            def count_folded(i, kk):
                act.wait_ge(folded, i * PAIR_CHUNKS + kk + 2)
                sums = work[:, kk % 4:kk % 4 + 2, :].rearrange("p s n -> p (s n)")
                m = i * (PAIR_CHUNKS // 2) + (kk - CHUNKS) // 2
                S.activation(sums, sums, ACT.Sign, accum_out=f_count[:, bass.ds(m, 1)]).then_inc(f_counted, 1)

            def filter(i, kk):
                act.wait_ge(turned, i * PAIR_CHUNKS + kk + 1)
                t = t_tiles[:, kk % T_RING, :]
                S.activation(t, t, ACT.Tanh).then_inc(filtered, 1)

            def relu(g, slot):
                act.wait_ge(used, T_RING + CHUNKS * (g + 1))
                act.wait_ge(feat_turned, g + 1)
                S.activation(feat[:, :], acc[:, slot, :], ACT.Relu, bias=bg_sb[:, :]).then_inc(feat_ready, 1)

            def pair(i, first):
                for kk in range(PAIR_CHUNKS):
                    h, c = divmod(kk, CHUNKS)
                    if first and h == 0:
                        count_first_group(kk)
                    elif not square_on_vector(i, kk):
                        square(i, kk)
                    if kk >= 1:
                        filter(i, kk - 1)
                    elif not first:
                        filter(i - 1, PAIR_CHUNKS - 1)
                    if kk % 2 == 1 and not (first and kk - 3 < CHUNKS):
                        count_folded(i, kk - 3)
                    if c == CHUNKS // 4 and not (first and h == 0):
                        relu(2 * i + h - 1, 1 - h)

            pair(0, True)
            with act.Fori(1, PAIRS) as i:
                pair(i, False)
            filter(PAIRS - 1, PAIR_CHUNKS - 1)
            count_folded(PAIRS - 1, PAIR_CHUNKS - 2)
            relu(GROUPS - 1, 1)

            act.wait_ge(flag_ready, 1)
            over = act.value_load(over_i[0:1, 0:1])
            for s in range(2):
                act.wait_ge(o_stored[s], 16 * PAIRS)
            out_tiles = out.rearrange("(t p) d -> t p d", p=D)
            with act.If(over > 0):
                with act.Fori(0, ROW_TILES) as t:
                    act.wait_ge(e_squared, t + 1)
                    S.activation(e_a, e_b, ACT.Tanh).then_inc(e_filtered, 1)
                    act.wait_ge(e_out, t + 2)
                    act.dma_start(out_tiles[bass.ds(t, 1)].rearrange("a p n -> (a p) n"), o_sb[:, 0, 0:D])\
                        .then_inc(e_stored, 16)
                    act.wait_ge(e_stored, 16 * t + 16)

        @block.tensor
        def _(pe):
            T = nc.tensor
            pe.sem_inc(used, T_RING)
            pe.sem_inc(folded, CHUNKS)
            pe.sem_inc(feat_turned, 1)
            pe.wait_ge(consts_loaded, 128)

            def project(s):
                pe.wait_ge(xt_copied, s + 1)
                if s >= 3:
                    pe.wait_ge(h2_ready, s - 2)
                T.matmul(work[:, 3 + s % 3, :], wp_sb[:, :], x_t[:, s % X_RING, :], start=True, stop=True)\
                    .then_inc(pre_ready, 1)

            for s in range(N // GROUP):
                if s * TILES % BLOCKS == 0:
                    pe.wait_ge(x_chunk_loaded[s * TILES // BLOCKS], 64)
                if s >= 3:
                    pe.wait_ge(xt_copied, s - 2)
                for t in range(TILES):
                    ins = T.transpose(work[:, s % 3, t * D:(t + 1) * D], x_all[:, (s * TILES + t) // BLOCKS, (s * TILES + t) % BLOCKS, :], eye_sb[:, :])
                ins.then_inc(xt_ready, 1)
                if s >= 1:
                    project(s - 1)
            project(N // GROUP - 1)
            for s in range(CHUNKS * BLOCKS // 4):
                if s == 0:
                    pe.wait_ge(h2_ready, N // GROUP)
                if s >= 6:
                    pe.wait_ge(g_copied, s - 5)
                for n in range(4):
                    m = 4 * s + n
                    ins = T.matmul(work[:, s % 6, n * D:(n + 1) * D], h2_t[:, m * D:(m + 1) * D], wg_sb[:, :],
                                   start=True, stop=True)
                ins.then_inc(g_ready, 1)
            pe.wait_ge(g_copied, CHUNKS * BLOCKS // 4)

            def fold_chunk(i, kk):
                wait_squared(pe, i, kk)
                pe.wait_ge(f_counted, i * (PAIR_CHUNKS // 2) + (kk - CHUNKS) // 2 + 1)
                upper = a_tiles[:, kk % A_RING, :].bitcast(BF16).rearrange("p (s n two) -> p s n two", n=GROUP, two=2)
                slices = STRIPS * QUARTER // GROUP
                for s in range(slices):
                    w = s % 4
                    ins = T.matmul(work[32 * w:32 * w + 32, kk % 4, :], fold_bf[:, :], upper[:, s, :, 1],
                                   start=(s < 4), stop=(s >= slices - 4))
                ins.then_inc(folded, 1)

            def multiply(i, kk):
                h, c = divmod(kk, CHUNKS)
                if c == 0 and not (isinstance(i, int) and i == 0):
                    pe.wait_ge(y_ready, 2 * i + h + 1)
                pe.wait_ge(filtered, i * PAIR_CHUNKS + kk + 1)
                for b in range(BLOCKS):
                    ins = T.matmul(acc[:, h, :], g_sb[:, c, b, :], t_tiles[:, kk % T_RING, b * GROUP:(b + 1) * GROUP],
                                   start=(c == 0 and b == 0), stop=(c == CHUNKS - 1 and b == BLOCKS - 1))
                ins.then_inc(used, 1)

            def turn_back(g, slot):
                pe.wait_ge(feat_ready, g + 1)
                for t in range(TILES):
                    ins = T.transpose(acc[:, slot, t * D:(t + 1) * D], feat[:, t * D:(t + 1) * D], eye_sb[:, :])
                ins.then_inc(feat_turned, 1)

            def pair(i, first):
                for kk in range(PAIR_CHUNKS):
                    h, c = divmod(kk, CHUNKS)
                    if not (first and h == 0):
                        fold_chunk(i, kk)
                    if kk >= 1:
                        multiply(i, kk - 1)
                    elif not first:
                        multiply(i - 1, PAIR_CHUNKS - 1)
                    if c == CHUNKS // 2 and not (first and h == 0):
                        turn_back(2 * i + h - 1, 1 - h)

            pe.wait_ge(fold_ready, 1)
            pair(0, True)
            with pe.Fori(1, PAIRS) as i:
                pair(i, False)
            multiply(PAIRS - 1, PAIR_CHUNKS - 1)

            pe.wait_ge(f_counted, 2 + COUNTS)
            T.matmul(work[:, 4, 0:CHUNKS * TILES], same_row_sb[:, :], a_count[:, :, :].rearrange("p c t -> p (c t)"),
                     start=True, stop=True).then_inc(bound_mm, 1)
            T.matmul(work[:, 5, 0:COUNTS], same_fold_sb[:, :], f_count[:, :], start=True, stop=True).then_inc(bound_mm, 1)
            turn_back(GROUPS - 1, 1)
            pe.wait_ge(bound_step, 3)
            T.transpose(work[0:1, 0, 0:D], bound_max[:, :], eye_sb[:, :]).then_inc(bound_turned, 1)

            pe.wait_ge(flag_ready, 1)
            over = pe.value_load(over_i[0:1, 0:1])
            with pe.If(over > 0):
                with pe.Fori(0, ROW_TILES) as t:
                    pe.wait_ge(e_kept, t + 1)
                    for n in range(ROW_TILES // 4):
                        if n >= 2:
                            pe.wait_ge(e_copied, t * (ROW_TILES // 4) + n - 1)
                        for w in range(4):
                            m = 4 * n + w
                            ins = T.transpose(work[:, n % 2, w * D:(w + 1) * D], e_f[:, m * D:(m + 1) * D], eye_sb[:, :])
                        ins.then_inc(e_turned, 1)
                    pe.wait_ge(e_copied, (t + 1) * (ROW_TILES // 4))
                    for n in range(ROW_TILES):
                        c, b = divmod(n, BLOCKS)
                        ins = T.matmul(acc[:, 0, 0:D], e_b[:, n * D:(n + 1) * D], g_sb[:, c, b, :],
                                       start=(n == 0), stop=(n == ROW_TILES - 1))
                    ins.then_inc(e_acc, 1)

        @block.gpsimd
        def _(pool):
            G = nc.gpsimd
            G.memset(minus_half[:, :], -0.5).then_inc(half_set, 1)
            pool.sem_inc(o_ready, 2)
            pool.wait_ge(half_set, 1)

            def normalise(g, slot, first):
                y = y_sb[:, slot, :].rearrange("p (t d) -> p t d", t=TILES)
                z = centred[:, :].rearrange("p (t d) -> p t d", t=TILES)
                pool.wait_ge(mv_ready, g + 2)
                G.tensor_tensor(z, y, mean[:, slot, :].unsqueeze(2).broadcast_to([D, TILES, D]), ALU.subtract)\
                    .then_inc(norm_step, 1)
                G.tensor_tensor(rstd[:, :], var_eps[:, slot, :], minus_half[:, :], ALU.pow).then_inc(norm_step, 1)
                if not first:
                    pool.wait_ge(o_stored[slot], 8 * (g - slot))
                pool.wait_ge(norm_step, 2 * g + 2)
                G.tensor_tensor(o_sb[:, slot, :].rearrange("p (t d) -> p t d", t=TILES), z,
                                rstd[:, :].unsqueeze(2).broadcast_to([D, TILES, D]), ALU.mult).then_inc(o_ready, 1)
                pool.wait_ge(o_ready, g + 3)
                pool.dma_start(out_rows[bass.ds(g, 1)].rearrange("a p t d -> (a p) t d"),
                               o_sb[:, slot, :].rearrange("p (t d) -> p t d", t=TILES)).then_inc(o_stored[slot], 16)

            for h in range(2):
                normalise(h, h, True)
            with pool.Fori(1, PAIRS) as i:
                for h in range(2):
                    normalise(2 * i + h, h, False)
            for s in range(2):
                pool.wait_ge(o_stored[s], 16 * PAIRS)

            pool.wait_ge(flag_ready, 1)
            over = pool.value_load(over_i[0:1, 0:1])
            with pool.If(over > 0):
                pool.sem_inc(e_out, 1)
                with pool.Fori(0, ROW_TILES) as t:
                    pool.wait_ge(e_mv, t + 1)
                    G.tensor_tensor(centred[:, 0:D], y_sb[:, 0, 0:D], mean[:, 0, 0:1].broadcast_to([D, D]),
                                    ALU.subtract).then_inc(e_pool, 1)
                    G.tensor_tensor(rstd[:, 0:1], var_eps[:, 0, 0:1], minus_half[:, 0:1], ALU.pow).then_inc(e_pool, 1)
                    pool.wait_ge(e_pool, 2 * t + 2)
                    G.tensor_tensor(o_sb[:, 0, 0:D], centred[:, 0:D], rstd[:, 0:1].broadcast_to([D, D]), ALU.mult)\
                        .then_inc(e_out, 1)


_INS = ["x", "adj", "L0_gnn_W_proj", "L0_gnn_b_proj", "L0_gnn_W_gcn", "L0_gnn_b_gcn"]


def kernel(**inputs):
    import numpy as np
    import concourse.bacc as bacc
    from concourse.bass_utils import run_bass_kernel_spmd

    nc = bacc.Bacc("TRN2", target_bir_lowering=False, num_devices=1)
    row = np.arange(D)
    arrays = {f"in_{name}": np.ascontiguousarray(inputs[name]) for name in _INS}
    arrays["in_eye"] = np.eye(D, dtype=np.float32)
    arrays["in_same_row"] = (row[:, None] % 32 == row[None, :] % 32).astype(np.float32)
    folded = 32 // FOLD_ROWS
    arrays["in_same_fold"] = ((row[:, None] // 32 == row[None, :] // 32)
                              & (row[:, None] % folded == row[None, :] % folded)).astype(np.float32)
    arrays["in_fold"] = (row[:, None] // FOLD_ROWS == row[None, :FOLDS]).astype(np.float32)
    args = [nc.dram_tensor(name, a.shape, mybir.dt.from_np(a.dtype), kind="ExternalInput").ap() for name, a in arrays.items()]
    out = nc.dram_tensor("out_dram", arrays["in_x"].shape, F32, kind="ExternalOutput").ap()
    build(nc, *args, out)
    return run_bass_kernel_spmd(nc, [arrays], core_ids=[0]).results[0]["out_dram"]
```

```python
from contextlib import ExitStack

import concourse.bass as bass
import concourse.mybir as mybir
from concourse.alu_op_type import AluOpType as ALU

F32 = mybir.dt.float32
BF16 = mybir.dt.bfloat16
I32 = mybir.dt.int32
ACT = mybir.ActivationFunctionType
AX = mybir.AxisListType

TOP = 350
EPS = 1e-5
D = 128
GROUP = 512
TILES = GROUP // D
CHUNK = 1024
QUARTER = CHUNK // 4
BLOCKS = CHUNK // D
STRIPS = GROUP // 32
A_RING = 4
T_RING = 4
FOLD_ROWS = 4
FOLDS = 128 // FOLD_ROWS
ON_VECTOR = 8
PRE_BEHIND, G_BEHIND = 2, 4
HEAD = 2
LEAD = 2
STEP_BITS = 30


def build(nc, x, adj, w_proj, b_proj, w_gcn, b_gcn, eye, same_row, same_fold, fold, out):
    N = x.shape[0]
    GROUPS = N // GROUP
    PAIRS = GROUPS // 2
    CHUNKS = N // CHUNK
    PAIR_CHUNKS = 2 * CHUNKS
    ROW_TILES = N // D
    RELU_AT, TURN_AT, FINISH_AT = CHUNKS // 4 + 1, CHUNKS // 2, 3 * CHUNKS // 4
    X_STEPS = N // GROUP
    COUNTS = (GROUPS - 1) * CHUNKS // 2
    assert CHUNKS % 4 == 0 and PAIRS >= 2

    ctx = ExitStack()
    with ctx:
        def sb(name, shape, dt=F32):
            return ctx.enter_context(nc.sbuf_tensor(name, shape, dt))

        def sem(name):
            return ctx.enter_context(nc.semaphore(name))

        a_tiles = sb("a_tiles", [D, A_RING, STRIPS * QUARTER])
        t_tiles = sb("t_tiles", [D, T_RING, BLOCKS * GROUP])
        g_sb = sb("g_sb", [D, CHUNKS, BLOCKS, D])
        junk = sb("junk", [D, TILES, STRIPS * QUARTER // TILES], BF16)
        x_sb = sb("x_sb", [D, 2, GROUP])
        feat = sb("feat", [D, GROUP])
        y_sb = sb("y_sb", [D, 2, GROUP])
        o_sb = sb("o_sb", [D, 2, GROUP])
        eye_sb = sb("eye_sb", [D, D])
        same_row_sb = sb("same_row_sb", [D, D])
        same_fold_sb = sb("same_fold_sb", [D, D])
        fold_sb = sb("fold_sb", [D, FOLDS])
        fold_bf = sb("fold_bf", [D, FOLDS], BF16)
        wp_sb = sb("wp_sb", [D, D])
        wg_sb = sb("wg_sb", [D, D])
        bp_sb = sb("bp_sb", [D, 1])
        bg_sb = sb("bg_sb", [D, 1])
        stats = sb("stats", [D, TILES, 6])
        mean = sb("mean", [D, 2, TILES])
        diff = sb("diff", [D, TILES])
        m2 = sb("m2", [D, TILES])
        var_eps = sb("var_eps", [D, 2, TILES])
        centred = sb("centred", [D, GROUP])
        rstd = sb("rstd", [D, TILES])
        minus_half = sb("minus_half", [D, TILES])
        a_count = sb("a_count", [D, CHUNKS, TILES])
        f_count = sb("f_count", [D, COUNTS])
        bound = sb("bound", [D, TILES + GROUPS - 1])
        bound_max = sb("bound_max", [D, 1])
        bound_all = sb("bound_all", [1, 1])
        over_i = sb("over_i", [1, 1], I32)

        x_all = g_sb
        x_t = sb("x_t", [D, 4, GROUP])
        h2_t = sb("h2_t", [D, 4, GROUP])

        acc = ctx.enter_context(nc.psum_tensor("acc", [D, 2, GROUP], F32))
        work = ctx.enter_context(nc.psum_tensor("work", [D, 6, GROUP], F32))

        eye_loaded = sem("eye_loaded")
        weights_loaded = sem("weights_loaded")
        consts_loaded = sem("consts_loaded")
        x_chunk_loaded = [sem(f"x_chunk_loaded{c}") for c in range(CHUNKS)]
        xt_ready = sem("xt_ready")
        xt_copied = sem("xt_copied")
        pre_ready = sem("pre_ready")
        h2_ready = sem("h2_ready")
        g_ready = sem("g_ready")
        g_copied = sem("g_copied")
        half_set = sem("half_set")
        a_loaded = [sem(f"a_loaded{s}") for s in range(A_RING)]
        x_loaded = [sem(f"x_loaded{s}") for s in range(2)]
        cut_ready = sem("cut_ready")
        squared_v = sem("squared_v")
        squared_s = sem("squared_s")
        turned = sem("turned")
        filtered = sem("filtered")
        used = sem("used")
        a_counted = sem("a_counted")
        folded = sem("folded")
        f_counted = sem("f_counted")
        fold_ready = sem("fold_ready")
        feat_ready = sem("feat_ready")
        feat_turned = sem("feat_turned")
        y_ready = sem("y_ready")
        stats_ready = sem("stats_ready")
        mv_ready = sem("mv_ready")
        norm_step = sem("norm_step")
        o_ready = sem("o_ready")
        o_stored = [sem(f"o_stored{s}") for s in range(2)]
        last_stored = sem("last_stored")
        bound_mm = sem("bound_mm")
        bound_step = sem("bound_step")
        bound_turned = sem("bound_turned")
        flag_ready = sem("flag_ready")
        e_loaded = sem("e_loaded")
        e_squared = sem("e_squared")
        e_filtered = sem("e_filtered")
        e_step = sem("e_step")
        e_kept = sem("e_kept")
        e_turned = sem("e_turned")
        e_copied = sem("e_copied")
        e_acc = sem("e_acc")
        e_y = sem("e_y")
        e_mv = sem("e_mv")
        e_pool = sem("e_pool")
        e_out = sem("e_out")
        e_stored = sem("e_stored")

        block = ctx.enter_context(nc.Block())

        adj_flat = adj.rearrange("r n -> (r n)")
        x_flat = x.rearrange("r d -> (r d)")
        out_rows = out.rearrange("(g t p) d -> g p t d", p=D, t=TILES)

        e_a, e_b = (a_tiles[:, 2 * n:2 * n + 2, :].rearrange("p s n -> p (s n)")[:, 0:N] for n in range(2))
        e_f = t_tiles[:, 0:2, :].rearrange("p s n -> p (s n)")[:, 0:N]

        on_vector = [kk % ON_VECTOR == 0 for kk in range(PAIR_CHUNKS)]
        on_vector_first = [kk < HEAD or on for kk, on in enumerate(on_vector)]
        on_vector_last = [CHUNKS <= kk < PAIR_CHUNKS - 1 or on for kk, on in enumerate(on_vector)]

        def is_pair(i, n):
            return isinstance(i, int) and i == n

        def kinds(i):
            return on_vector_first if is_pair(i, 0) else on_vector_last if is_pair(i, PAIRS - 1) else on_vector

        def square_on_vector(i, kk):
            return kinds(i)[kk]

        def squares_of_kind(i, kk):
            kind = kinds(i)[kk]
            here = kinds(i)[:kk + 1].count(kind)
            if is_pair(i, 0):
                return here
            return i * on_vector.count(kind) + (on_vector_first.count(kind) - on_vector.count(kind) + here)

        def wait_squared(engine, i, kk):
            engine.wait_ge(squared_v if square_on_vector(i, kk) else squared_s, squares_of_kind(i, kk))

        EXACT_STEPS = 2 + 6 * STEP_BITS + 11
        thr_i = sb("thr_i", [D, 1], I32)
        cand_i = sb("cand_i", [D, 1], I32)
        bit_i = sb("bit_i", [D, 1], I32)
        ok_i = sb("ok_i", [D, 1], I32)
        cnt = sb("cnt", [D, 1])
        need = sb("need", [D, 1])

        def exact_rows(dve, V, moments):
            with dve.Fori(0, ROW_TILES) as t:
                base = t * EXACT_STEPS
                thr_f, cand_f = thr_i[:, :].bitcast(F32), cand_i[:, :].bitcast(F32)
                dve.wait_ge(e_loaded, 48 * t + 48)
                V.scalar_tensor_tensor(e_b, e_a, 0.0, e_a, ALU.max, ALU.mult).then_inc(e_squared, 1)
                dve.wait_ge(e_filtered, t + 1)
                V.memset(thr_i[:, :], 0).then_inc(e_step, 1)
                V.memset(bit_i[:, :], 1 << (STEP_BITS - 1)).then_inc(e_step, 1)
                with dve.Fori(0, STEP_BITS) as b:
                    at = base + 2 + 6 * b
                    dve.wait_ge(e_step, at)
                    V.tensor_tensor(cand_i[:, :], thr_i[:, :], bit_i[:, :], ALU.bitwise_or).then_inc(e_step, 1)
                    dve.wait_ge(e_step, at + 1)
                    V.tensor_scalar(e_f, e_a, cand_f, None, ALU.is_ge, ALU.add, accum_out=cnt[:, :]).then_inc(e_step, 1)
                    dve.wait_ge(e_step, at + 2)
                    V.tensor_scalar(ok_i[:, :], cnt[:, :], float(TOP), -1.0, ALU.is_ge, ALU.mult).then_inc(e_step, 1)
                    dve.wait_ge(e_step, at + 3)
                    V.tensor_tensor(ok_i[:, :], ok_i[:, :], bit_i[:, :], ALU.bitwise_and).then_inc(e_step, 1)
                    dve.wait_ge(e_step, at + 4)
                    V.tensor_tensor(thr_i[:, :], thr_i[:, :], ok_i[:, :], ALU.bitwise_or).then_inc(e_step, 1)
                    V.tensor_single_scalar(bit_i[:, :], bit_i[:, :], 1, ALU.logical_shift_right).then_inc(e_step, 1)
                at = base + 2 + 6 * STEP_BITS
                dve.wait_ge(e_step, at)
                V.tensor_scalar(e_f, e_a, thr_f, None, ALU.is_gt, ALU.add, accum_out=cnt[:, :]).then_inc(e_step, 1)
                dve.wait_ge(e_step, at + 1)
                V.tensor_scalar(need[:, :], cnt[:, :], -1.0, float(TOP), ALU.mult, ALU.add).then_inc(e_step, 1)
                V.tensor_scalar(e_f, e_a, thr_f, None, ALU.is_equal).then_inc(e_step, 1)
                dve.wait_ge(e_step, at + 3)
                V.tensor_tensor_scan(e_b, e_f, e_f, 0.0, ALU.add, ALU.max).then_inc(e_step, 1)
                dve.wait_ge(e_step, at + 4)
                V.scalar_tensor_tensor(e_f, e_b, need[:, :], e_f, ALU.is_le, ALU.mult).then_inc(e_step, 1)
                dve.wait_ge(e_step, at + 5)
                V.scalar_tensor_tensor(e_b, e_a, thr_f, e_f, ALU.is_gt, ALU.add).then_inc(e_step, 1)
                dve.wait_ge(e_step, at + 6)
                for c in range(CHUNKS):
                    lo, hi = c * CHUNK, (c + 1) * CHUNK
                    ins = V.tensor_tensor(e_f[:, lo:hi].rearrange("p (b q r) -> p q b r", q=4, r=32),
                                          e_a[:, lo:hi].rearrange("p (q b r) -> p q b r", q=4, r=32),
                                          e_b[:, lo:hi].rearrange("p (q b r) -> p q b r", q=4, r=32), ALU.mult)
                ins.then_inc(e_kept, 1)
                for n in range(ROW_TILES // 4):
                    m = t * (ROW_TILES // 4) + n
                    dve.wait_ge(e_turned, m + 1)
                    if n == 0:
                        dve.wait_ge(e_kept, t + 1)
                    V.tensor_copy(e_b[:, n * GROUP:(n + 1) * GROUP], work[:, n % 2, :]).then_inc(e_copied, 1)
                dve.wait_ge(e_acc, t + 1)
                V.tensor_tensor(feat[:, 0:D], acc[:, 0, 0:D], x_sb[:, 1, 0:D], ALU.add).then_inc(e_y, 1)
                dve.wait_ge(e_y, 2 * t + 1)
                V.scalar_tensor_tensor(y_sb[:, 0, 0:D], feat[:, 0:D], 0.0, x_sb[:, 0, 0:D], ALU.max, ALU.add)\
                    .then_inc(e_y, 1)
                dve.wait_ge(e_y, 2 * t + 2)
                V.bn_stats(stats[:, 0, :], y_sb[:, 0, 0:D]).then_inc(e_step, 1)
                moments(e_step, at + 7, 0, 1, e_mv)

        @block.sync
        def _(sp):
            sp.dma_start(eye_sb[:, :], eye).then_inc(eye_loaded, 16)

            def load_x_chunk(c):
                for q in range(4):
                    at = c * CHUNK + q * QUARTER
                    sp.dma_start(x_all[32 * q:32 * q + 32, c, :, :],
                                 x[at:at + QUARTER, :].rearrange("(b r) d -> r b d", r=32))\
                        .then_inc(x_chunk_loaded[c], 16)

            def load_chunk(strips, kk):
                for q in range(4):
                    at = kk % CHUNKS * CHUNK + q * QUARTER
                    sp.dma_start(a_tiles[32 * q:32 * q + 32, kk % A_RING, :].rearrange("c (i n) -> c i n", i=STRIPS),
                                 strips[:, :, at:at + QUARTER]).then_inc(a_loaded[kk % A_RING], 16)

            def load_pair(i, loaded):
                for h in range(2):
                    g = 2 * i + h
                    adj_at, x_at = (g * -(GROUP * w) + (GROUPS - 1) * GROUP * w for w in (N, D))
                    if not isinstance(i, int):
                        adj_at, x_at = sp.snap(adj_at), sp.snap(x_at)
                    strips = adj_flat[bass.ds(adj_at, GROUP * N)].rearrange("(i c n) -> c i n", c=32, n=N)
                    for c in range(CHUNKS):
                        kk = h * CHUNKS + c
                        k = i * PAIR_CHUNKS + kk
                        if not is_pair(i, 0) or kk >= A_RING:
                            if is_pair(i, PAIRS - 1) and kk - A_RING >= CHUNKS:
                                sp.wait_ge(a_counted, kk - A_RING - CHUNKS + 1)
                            else:
                                sp.wait_ge(folded, k - (A_RING - 1))
                            sp.wait_ge(turned, k - (A_RING - 1))
                        if not is_pair(i, 0) or kk >= loaded:
                            load_chunk(strips, kk)
                        if c == CHUNKS // 4:
                            sp.wait_ge(y_ready, g + 1)
                            sp.dma_start(x_sb[:, h, :].rearrange("p (t d) -> p t d", t=TILES),
                                         x_flat[bass.ds(x_at, GROUP * D)].rearrange("(t p d) -> p t d", p=D, d=D))\
                                .then_inc(x_loaded[h], 16)

            first_strips = adj_flat[(GROUPS - 1) * GROUP * N:].rearrange("(i c n) -> c i n", c=32, n=N)
            for c in range(CHUNKS):
                load_x_chunk(c)
                if c == 1:
                    for dst, src in ((wp_sb[:, :], w_proj), (bp_sb[:, :], b_proj.rearrange("(d a) -> d a", a=1)),
                                     (wg_sb[:, :], w_gcn)):
                        sp.dma_start(dst, src).then_inc(weights_loaded, 16)
                if c == 3:
                    for dst, src in ((bg_sb[:, :], b_gcn.rearrange("(d a) -> d a", a=1)), (fold_sb[:, :], fold),
                                     (same_row_sb[:, :], same_row), (same_fold_sb[:, :], same_fold)):
                        sp.dma_start(dst, src).then_inc(consts_loaded, 16)
                if c == CHUNKS // 2:
                    load_chunk(first_strips, 0)
            load_pair(0, 1)
            with sp.Fori(1, PAIRS - 1) as i:
                load_pair(i, 0)
            load_pair(PAIRS - 1, 0)
            sp.wait_ge(o_ready, 2 + GROUPS)
            sp.dma_start(out_rows[0], o_sb[:, 1, :].rearrange("p (t d) -> p t d", t=TILES)).then_inc(last_stored, 16)

            sp.wait_ge(flag_ready, 1)
            over = sp.value_load(over_i[0:1, 0:1])
            with sp.If(over > 0):
                adj_tiles = adj.rearrange("(t p) n -> t p n", p=D)
                x_tiles = x.rearrange("(t p) d -> t p d", p=D)
                with sp.Fori(0, ROW_TILES) as t:
                    sp.wait_ge(e_out, t + 1)
                    sp.dma_start(e_a, adj_tiles[bass.ds(t, 1)].rearrange("a p n -> (a p) n")).then_inc(e_loaded, 16)
                    sp.dma_start(x_sb[:, 0, 0:D], x_tiles[bass.ds(t, 1)].rearrange("a p n -> (a p) n"))\
                        .then_inc(e_loaded, 16)
                    sp.dma_start(x_sb[:, 1, 0:D], b_gcn.rearrange("(a d) -> a d", a=1).broadcast_to([D, D]))\
                        .then_inc(e_loaded, 16)

        @block.vector
        def _(dve):
            V = nc.vector
            dve.wait_ge(consts_loaded, 64)
            V.tensor_copy(fold_bf[:, :], fold_sb[:, :]).then_inc(fold_ready, 1)

            def finish(g, slot):
                dve.wait_ge(feat_turned, g + 2)
                dve.wait_ge(x_loaded[slot], 8 * (g - slot) + 16)
                dve.wait_ge(o_ready, g + 1)
                V.tensor_tensor(y_sb[:, slot, :], acc[:, slot, :], x_sb[:, slot, :], ALU.add).then_inc(y_ready, 1)
                dve.wait_ge(y_ready, g + 3)
                dve.wait_ge(mv_ready, g + 1)
                for t in range(TILES):
                    V.bn_stats(stats[:, t, :], y_sb[:, slot, t * D:(t + 1) * D]).then_inc(stats_ready, 1)
                moments(stats_ready, (TILES + 4) * g + TILES, slot, TILES, mv_ready)

            def moments(step, at, slot, tiles, done):
                half = stats[:, 0:tiles, :]
                dve.wait_ge(step, at)
                V.tensor_tensor(mean[:, slot, 0:tiles], half[:, :, 1], half[:, :, 4], ALU.add).then_inc(step, 1)
                V.tensor_tensor(diff[:, 0:tiles], half[:, :, 1], half[:, :, 4], ALU.subtract).then_inc(step, 1)
                V.tensor_tensor(m2[:, 0:tiles], half[:, :, 2], half[:, :, 5], ALU.add).then_inc(step, 1)
                dve.wait_ge(step, at + 3)
                V.tensor_scalar(mean[:, slot, 0:tiles], mean[:, slot, 0:tiles], 0.5, None, ALU.mult)
                V.scalar_tensor_tensor(diff[:, 0:tiles], diff[:, 0:tiles], 0.25, diff[:, 0:tiles], ALU.mult, ALU.mult)
                V.tensor_scalar(m2[:, 0:tiles], m2[:, 0:tiles], 1.0 / D, EPS, ALU.mult, ALU.add).then_inc(step, 1)
                dve.wait_ge(step, at + 4)
                V.tensor_tensor(var_eps[:, slot, 0:tiles], m2[:, 0:tiles], diff[:, 0:tiles], ALU.add).then_inc(done, 1)

            def square(i, kk):
                a = a_tiles[:, kk % A_RING, :]
                dve.wait_ge(a_loaded[kk % A_RING], i * (64 * PAIR_CHUNKS // A_RING) + 64 * (kk // A_RING + 1))
                if square_on_vector(i, kk):
                    V.scalar_tensor_tensor(a, a, 0.0, a, ALU.max, ALU.mult).then_inc(squared_v, 1)
                else:
                    V.tensor_scalar(a, a, 0.0, None, ALU.max).then_inc(cut_ready, 1)

            def turn(i, kk):
                wait_squared(dve, i, kk)
                dve.wait_ge(used, i * PAIR_CHUNKS + kk + 1)
                V.transpose(t_tiles[:, kk % T_RING, :].rearrange("p (b i r) -> p i b r", i=STRIPS, r=32),
                            a_tiles[:, kk % A_RING, :].rearrange("p (i b r) -> p i b r", i=STRIPS, r=32)).then_inc(turned, 1)

            def pair(i, first, last):
                for kk in range(PAIR_CHUNKS):
                    h, c = divmod(kk, CHUNKS)
                    square(i, kk)
                    if first and kk == 0:
                        turn(i, kk)
                    elif kk >= 1 and not (first and kk == 1):
                        turn(i, kk - 1)
                    elif not first:
                        turn(i - 1, PAIR_CHUNKS - 1)
                    if c == FINISH_AT and not (first and h == 0) and not (last and h == 1):
                        finish(2 * i + h - 1, 1 - h)

            dve.sem_inc(y_ready, 2)
            dve.sem_inc(mv_ready, 1)
            pair(0, True, False)
            with dve.Fori(1, PAIRS - 1) as i:
                pair(i, False, False)
            pair(PAIRS - 1, False, True)
            turn(PAIRS - 1, PAIR_CHUNKS - 1)

            finish(GROUPS - 2, 0)

            dve.wait_ge(bound_mm, 2)
            V.tensor_reduce(bound[:, 0:TILES], work[:, 4, 0:CHUNKS * TILES].rearrange("p (c t) -> p t c", t=TILES),
                            AX.X, ALU.add).then_inc(bound_step, 1)
            V.tensor_reduce(bound[:, TILES:], work[:, 5, 0:COUNTS].rearrange("p (g c) -> p g c", c=CHUNKS // 2),
                            AX.X, ALU.add).then_inc(bound_step, 1)
            dve.wait_ge(bound_step, 2)
            V.tensor_reduce(bound_max[:, :], bound[:, :], AX.X, ALU.max).then_inc(bound_step, 1)

            finish(GROUPS - 1, 1)
            dve.wait_ge(norm_step, 2 * GROUPS - 1)
            dve.wait_ge(o_stored[1], 16 * (PAIRS - 1))
            for t in range(TILES):
                ins = V.tensor_scalar(o_sb[:, 1, t * D:(t + 1) * D], y_sb[:, 1, t * D:(t + 1) * D], mean[:, 1, t:t + 1],
                                      rstd[:, t:t + 1], ALU.subtract, ALU.mult)
            ins.then_inc(o_ready, 1)
            dve.wait_ge(bound_turned, 1)
            V.tensor_reduce(bound_all[:, :], work[0:1, 0, 0:D], AX.X, ALU.max).then_inc(bound_step, 1)
            dve.wait_ge(bound_step, 4)
            V.tensor_scalar(over_i[:, :], bound_all[:, :], TOP + 0.5, None, ALU.is_gt).then_inc(flag_ready, 1)

            dve.wait_ge(flag_ready, 1)
            over = dve.value_load(over_i[0:1, 0:1])
            dve.wait_ge(o_ready, 2 + GROUPS)
            with dve.If(over > 0):
                exact_rows(dve, V, moments)

        @block.scalar
        def _(act):
            S = nc.scalar
            act.sem_inc(f_counted, 2)
            def square(i, kk):
                act.wait_ge(cut_ready, squares_of_kind(i, kk))
                a = a_tiles[:, kk % A_RING, :]
                S.activation(a, a, ACT.Square).then_inc(squared_s, 1)

            def count_last_group(kk):
                c = kk - CHUNKS
                wait_squared(act, PAIRS - 1, kk)
                if c >= 1:
                    act.wait_ge(a_counted, c)
                rows = a_tiles[:, kk % A_RING, :].rearrange("p (t n) -> p t n", t=TILES)
                for t in range(TILES):
                    ins = S.activation(junk[:, t, :], rows[:, t, :], ACT.Sign, accum_out=a_count[:, c, t:t + 1])
                ins.then_inc(a_counted, 1)

            def count_folded(i, kk):
                act.wait_ge(folded, i * PAIR_CHUNKS + kk + 2)
                sums = work[:, kk % 4:kk % 4 + 2, :].rearrange("p s n -> p (s n)")
                m = i * (PAIR_CHUNKS // 2) + kk // 2
                S.activation(sums, sums, ACT.Sign, accum_out=f_count[:, bass.ds(m, 1)]).then_inc(f_counted, 1)

            def filter(i, kk):
                act.wait_ge(turned, i * PAIR_CHUNKS + kk + 1)
                t = t_tiles[:, kk % T_RING, :]
                S.activation(t, t, ACT.Tanh).then_inc(filtered, 1)

            def relu(g, slot):
                act.wait_ge(used, T_RING + CHUNKS * (g + 1))
                act.wait_ge(feat_turned, g + 1)
                S.activation(feat[:, :], acc[:, slot, :], ACT.Relu, bias=bg_sb[:, :]).then_inc(feat_ready, 1)

            g_flat = g_sb[:, :, :, :].rearrange("p c b d -> p (c b d)")
            head_steps = (X_STEPS - 4, X_STEPS + G_BEHIND - 1)
            for s in range(X_STEPS + G_BEHIND):
                if s < X_STEPS:
                    act.wait_ge(xt_ready, s + 1)
                    if s >= 4:
                        act.wait_ge(pre_ready, s - 3)
                    S.activation(x_t[:, s % 4, :], work[:, s % 3, :], ACT.Copy).then_inc(xt_copied, 1)
                m = s - PRE_BEHIND
                if 0 <= m < X_STEPS:
                    if m == 0:
                        act.wait_ge(weights_loaded, 48)
                    act.wait_ge(pre_ready, m + 1)
                    if m >= 4:
                        act.wait_ge(g_ready, m - 3)
                    S.activation(h2_t[:, m % 4, :], work[:, 3 + m % 3, :], ACT.Tanh, bias=bp_sb[:, :]).then_inc(h2_ready, 1)
                m = s - G_BEHIND
                if m >= 0:
                    act.wait_ge(g_ready, m + 1)
                    S.activation(g_flat[:, m * GROUP:(m + 1) * GROUP], acc[:, m % 2, :], ACT.Copy).then_inc(g_copied, 1)
                if s in head_steps:
                    filter(0, head_steps.index(s))
            act.wait_ge(consts_loaded, 64)

            def pair(i, first, last):
                for kk in range(PAIR_CHUNKS):
                    h, c = divmod(kk, CHUNKS)
                    if not square_on_vector(i, kk):
                        square(i, kk)
                    if last and h == 1 and c < CHUNKS - 1:
                        count_last_group(kk)
                    if kk >= 1 and not (first and kk <= HEAD):
                        filter(i, kk - 1)
                    elif not first:
                        filter(i - 1, PAIR_CHUNKS - 1)
                    if kk % 2 == 1 and not (first and kk < 3) and not (last and kk - 3 >= CHUNKS):
                        count_folded(i, kk - 3)
                    if c == RELU_AT and not (first and h == 0):
                        relu(2 * i + h - 1, 1 - h)

            pair(0, True, False)
            with act.Fori(1, PAIRS - 1) as i:
                pair(i, False, False)
            pair(PAIRS - 1, False, True)
            filter(PAIRS - 1, PAIR_CHUNKS - 1)
            count_last_group(PAIR_CHUNKS - 1)
            relu(GROUPS - 1, 1)

            act.wait_ge(flag_ready, 1)
            over = act.value_load(over_i[0:1, 0:1])
            for s in range(2):
                act.wait_ge(o_stored[s], 16 * (PAIRS - s))
            act.wait_ge(last_stored, 16)
            out_tiles = out.rearrange("(t p) d -> t p d", p=D)
            with act.If(over > 0):
                with act.Fori(0, ROW_TILES) as t:
                    act.wait_ge(e_squared, t + 1)
                    S.activation(e_a, e_b, ACT.Tanh).then_inc(e_filtered, 1)
                    act.wait_ge(e_out, t + 2)
                    act.dma_start(out_tiles[bass.ds(t, 1)].rearrange("a p n -> (a p) n"), o_sb[:, 0, 0:D])\
                        .then_inc(e_stored, 16)
                    act.wait_ge(e_stored, 16 * t + 16)

        @block.tensor
        def _(pe):
            T = nc.tensor
            pe.sem_inc(used, T_RING)
            pe.sem_inc(feat_turned, 1)
            pe.wait_ge(eye_loaded, 16)
            for s in range(X_STEPS + G_BEHIND):
                if s < X_STEPS:
                    if s * TILES % BLOCKS == 0:
                        pe.wait_ge(x_chunk_loaded[s * TILES // BLOCKS], 64)
                    if s >= 3:
                        pe.wait_ge(xt_copied, s - 2)
                    for t in range(TILES):
                        c, b = divmod(s * TILES + t, BLOCKS)
                        ins = T.transpose(work[:, s % 3, t * D:(t + 1) * D], x_all[:, c, b, :], eye_sb[:, :])
                    ins.then_inc(xt_ready, 1)
                m = s - PRE_BEHIND
                if 0 <= m < X_STEPS:
                    if m == 0:
                        pe.wait_ge(weights_loaded, 48)
                    pe.wait_ge(xt_copied, m + 1)
                    if m >= 3:
                        pe.wait_ge(h2_ready, m - 2)
                    T.matmul(work[:, 3 + m % 3, :], wp_sb[:, :], x_t[:, m % 4, :], start=True, stop=True)\
                        .then_inc(pre_ready, 1)
                m = s - G_BEHIND
                if m >= 0:
                    pe.wait_ge(h2_ready, m + 1)
                    if m >= 2:
                        pe.wait_ge(g_copied, m - 1)
                    for n in range(TILES):
                        ins = T.matmul(acc[:, m % 2, n * D:(n + 1) * D], h2_t[:, m % 4, n * D:(n + 1) * D],
                                       wg_sb[:, :], start=True, stop=True)
                    ins.then_inc(g_ready, 1)
            pe.wait_ge(consts_loaded, 64)
            pe.wait_ge(g_copied, X_STEPS)

            def fold_chunk(i, kk):
                wait_squared(pe, i, kk)
                if kk % 2 == 0:
                    pe.wait_ge(f_counted, i * (PAIR_CHUNKS // 2) + kk // 2 + 1)
                upper = a_tiles[:, kk % A_RING, :].bitcast(BF16).rearrange("p (s n two) -> p s n two", n=GROUP, two=2)
                slices = STRIPS * QUARTER // GROUP
                for s in range(slices):
                    w = s % 4
                    ins = T.matmul(work[32 * w:32 * w + 32, kk % 4, :], fold_bf[:, :], upper[:, s, :, 1],
                                   start=(s < 4), stop=(s >= slices - 4))
                ins.then_inc(folded, 1)

            def multiply(i, kk):
                h, c = divmod(kk, CHUNKS)
                if c == 0 and not (isinstance(i, int) and i == 0):
                    pe.wait_ge(y_ready, 2 * i + h + 1)
                pe.wait_ge(filtered, i * PAIR_CHUNKS + kk + 1)
                for b in range(BLOCKS):
                    ins = T.matmul(acc[:, h, :], g_sb[:, c, b, :], t_tiles[:, kk % T_RING, b * GROUP:(b + 1) * GROUP],
                                   start=(c == 0 and b == 0), stop=(c == CHUNKS - 1 and b == BLOCKS - 1))
                ins.then_inc(used, 1)

            def turn_back(g, slot):
                pe.wait_ge(feat_ready, g + 1)
                for t in range(TILES):
                    ins = T.transpose(acc[:, slot, t * D:(t + 1) * D], feat[:, t * D:(t + 1) * D], eye_sb[:, :])
                ins.then_inc(feat_turned, 1)

            def pair(i, first, last):
                for kk in range(PAIR_CHUNKS):
                    h, c = divmod(kk, CHUNKS)
                    if not (last and h == 1):
                        fold_chunk(i, kk)
                    if first and kk <= CHUNKS:
                        if 1 <= kk < CHUNKS:
                            multiply(i, kk - 1)
                    elif kk >= LEAD:
                        multiply(i, kk - LEAD)
                    else:
                        multiply(i - 1, PAIR_CHUNKS + kk - LEAD)
                    if c == TURN_AT and not (first and h == 0):
                        turn_back(2 * i + h - 1, 1 - h)

            pe.wait_ge(fold_ready, 1)
            pair(0, True, False)
            with pe.Fori(1, PAIRS - 1) as i:
                pair(i, False, False)
            pair(PAIRS - 1, False, True)
            for kk in range(PAIR_CHUNKS - LEAD, PAIR_CHUNKS):
                multiply(PAIRS - 1, kk)

            pe.wait_ge(f_counted, 2 + COUNTS)
            pe.wait_ge(a_counted, CHUNKS)
            T.matmul(work[:, 4, 0:CHUNKS * TILES], same_row_sb[:, :], a_count[:, :, :].rearrange("p c t -> p (c t)"),
                     start=True, stop=True).then_inc(bound_mm, 1)
            T.matmul(work[:, 5, 0:COUNTS], same_fold_sb[:, :], f_count[:, :], start=True, stop=True).then_inc(bound_mm, 1)
            turn_back(GROUPS - 1, 1)
            pe.wait_ge(bound_step, 3)
            T.transpose(work[0:1, 0, 0:D], bound_max[:, :], eye_sb[:, :]).then_inc(bound_turned, 1)

            pe.wait_ge(flag_ready, 1)
            over = pe.value_load(over_i[0:1, 0:1])
            with pe.If(over > 0):
                with pe.Fori(0, ROW_TILES) as t:
                    pe.wait_ge(e_kept, t + 1)
                    for n in range(ROW_TILES // 4):
                        if n >= 2:
                            pe.wait_ge(e_copied, t * (ROW_TILES // 4) + n - 1)
                        for w in range(4):
                            m = 4 * n + w
                            ins = T.transpose(work[:, n % 2, w * D:(w + 1) * D], e_f[:, m * D:(m + 1) * D], eye_sb[:, :])
                        ins.then_inc(e_turned, 1)
                    pe.wait_ge(e_copied, (t + 1) * (ROW_TILES // 4))
                    for n in range(ROW_TILES):
                        c, b = divmod(n, BLOCKS)
                        ins = T.matmul(acc[:, 0, 0:D], e_b[:, n * D:(n + 1) * D], g_sb[:, c, b, :],
                                       start=(n == 0), stop=(n == ROW_TILES - 1))
                    ins.then_inc(e_acc, 1)

        @block.gpsimd
        def _(pool):
            G = nc.gpsimd
            G.memset(minus_half[:, :], -0.5).then_inc(half_set, 1)
            pool.sem_inc(o_ready, 2)
            pool.wait_ge(half_set, 1)

            def normalise(g, slot, first):
                place = GROUPS - 1 - g if first else pool.snap(g * -1 + (GROUPS - 1))
                y = y_sb[:, slot, :].rearrange("p (t d) -> p t d", t=TILES)
                z = centred[:, :].rearrange("p (t d) -> p t d", t=TILES)
                pool.wait_ge(mv_ready, g + 2)
                G.tensor_tensor(z, y, mean[:, slot, :].unsqueeze(2).broadcast_to([D, TILES, D]), ALU.subtract)\
                    .then_inc(norm_step, 1)
                G.tensor_tensor(rstd[:, :], var_eps[:, slot, :], minus_half[:, :], ALU.pow).then_inc(norm_step, 1)
                if not first:
                    pool.wait_ge(o_stored[slot], 8 * (g - slot))
                pool.wait_ge(norm_step, 2 * g + 2)
                G.tensor_tensor(o_sb[:, slot, :].rearrange("p (t d) -> p t d", t=TILES), z,
                                rstd[:, :].unsqueeze(2).broadcast_to([D, TILES, D]), ALU.mult).then_inc(o_ready, 1)
                pool.wait_ge(o_ready, g + 3)
                pool.dma_start(out_rows[bass.ds(place, 1)].rearrange("a p t d -> (a p) t d"),
                               o_sb[:, slot, :].rearrange("p (t d) -> p t d", t=TILES)).then_inc(o_stored[slot], 16)

            for h in range(2):
                normalise(h, h, True)
            with pool.Fori(1, PAIRS - 1) as i:
                for h in range(2):
                    normalise(2 * i + h, h, False)
            normalise(GROUPS - 2, 0, False)
            pool.wait_ge(mv_ready, GROUPS + 1)
            G.tensor_tensor(rstd[:, :], var_eps[:, 1, :], minus_half[:, :], ALU.pow).then_inc(norm_step, 1)
            for s in range(2):
                pool.wait_ge(o_stored[s], 16 * (PAIRS - s))

            pool.wait_ge(flag_ready, 1)
            over = pool.value_load(over_i[0:1, 0:1])
            with pool.If(over > 0):
                pool.sem_inc(e_out, 1)
                with pool.Fori(0, ROW_TILES) as t:
                    pool.wait_ge(e_mv, t + 1)
                    G.tensor_tensor(centred[:, 0:D], y_sb[:, 0, 0:D], mean[:, 0, 0:1].broadcast_to([D, D]),
                                    ALU.subtract).then_inc(e_pool, 1)
                    G.tensor_tensor(rstd[:, 0:1], var_eps[:, 0, 0:1], minus_half[:, 0:1], ALU.pow).then_inc(e_pool, 1)
                    pool.wait_ge(e_pool, 2 * t + 2)
                    G.tensor_tensor(o_sb[:, 0, 0:D], centred[:, 0:D], rstd[:, 0:1].broadcast_to([D, D]), ALU.mult)\
                        .then_inc(e_out, 1)


_INS = ["x", "adj", "L0_gnn_W_proj", "L0_gnn_b_proj", "L0_gnn_W_gcn", "L0_gnn_b_gcn"]


def kernel(**inputs):
    import numpy as np
    import concourse.bacc as bacc
    from concourse.bass_utils import run_bass_kernel_spmd

    nc = bacc.Bacc("TRN2", target_bir_lowering=False, num_devices=1)
    row = np.arange(D)
    arrays = {f"in_{name}": np.ascontiguousarray(inputs[name]) for name in _INS}
    arrays["in_eye"] = np.eye(D, dtype=np.float32)
    arrays["in_same_row"] = (row[:, None] % 32 == row[None, :] % 32).astype(np.float32)
    folded = 32 // FOLD_ROWS
    arrays["in_same_fold"] = ((row[:, None] // 32 == row[None, :] // 32)
                              & (row[:, None] % folded == row[None, :] % folded)).astype(np.float32)
    arrays["in_fold"] = (row[:, None] // FOLD_ROWS == row[None, :FOLDS]).astype(np.float32)
    args = [nc.dram_tensor(name, a.shape, mybir.dt.from_np(a.dtype), kind="ExternalInput").ap() for name, a in arrays.items()]
    out = nc.dram_tensor("out_dram", arrays["in_x"].shape, F32, kind="ExternalOutput").ap()
    build(nc, *args, out)
    return run_bass_kernel_spmd(nc, [arrays], core_ids=[0]).results[0]["out_dram"]
```
